# Optimizing a Trainium2 kernel written in Bass

```python
import numpy as np
import jax
import jax.numpy as jnp

def _softmax(x, axis=-1):
    return jax.nn.softmax(x, axis=axis)

def _gelu(x):
    return jax.nn.gelu(x, approximate=True)

def _silu(x):
    return jax.nn.silu(x)

def _sigmoid(x):
    return jax.nn.sigmoid(x)

def _layernorm(x, axis=-1, eps=1e-05):
    m = jnp.mean(x, axis=axis, keepdims=True)
    v = jnp.var(x, axis=axis, keepdims=True)
    return (x - m) / jnp.sqrt(v + eps)

def _scatter_add(tgt, idx, src, axis=0):
    return tgt.at[idx].add(src)

def _segment_sum(src, seg, n):
    return jax.ops.segment_sum(src, seg, n)
kernel_name = 'mk_flamingo_gated_d1_seqx_r8_ede6bd'

def setup_inputs(seed: int=0):
    np.random.seed(seed)
    _w = jnp.asarray

    def _rec_inputs():
        import jax
        import jax.numpy as jnp
        _rk = jax.random.key(seed)
        x = -0.0002928 + 1 * jax.random.normal(jax.random.fold_in(_rk, 1), (2, 512, 128), jnp.float32)
        _lenS = 512 - jax.random.randint(jax.random.fold_in(_rk, 7), (2,), 0, max(1, 512 // 4) + 1, jnp.int32)
        _lenS2 = 77 - jax.random.randint(jax.random.fold_in(_rk, 8), (2,), 0, max(1, 77 // 4) + 1, jnp.int32)
        _ctx_1024P = jax.random.normal(jax.random.fold_in(_rk, 11), (2, 16, 128), jnp.float32)
        _ctx_1024c = jax.random.dirichlet(jax.random.fold_in(_rk, 511), 0.3 * jnp.ones((16,), jnp.float32), (2, 77))
        _ctx_1024t = jnp.einsum('bsk,bkd->bsd', _ctx_1024c, _ctx_1024P)
        _ctx_1024t = _ctx_1024t * jax.lax.rsqrt(jnp.mean(jnp.square(_ctx_1024t)) + 1e-12) * 0.953939
        ctx_1024 = -1.39393e-06 + 0.999914 * (_ctx_1024t + 0.3 * jax.random.normal(jax.random.fold_in(_rk, 611), (2, 77, 128), jnp.float32))
        fside_BxSxS2_0 = jax.random.uniform(jax.random.fold_in(_rk, 12), (2, 512, 77), jnp.float32, 0.0, 1)
        _validS = jnp.arange(512)[None, :] < _lenS[:, None]
        _validS2 = jnp.arange(77)[None, :] < _lenS2[:, None]
        _causal = jnp.tril(jnp.ones((512, 512), dtype=bool))
        mask_BxSxS2_ik1 = jnp.where(jnp.broadcast_to(_validS2[:, None, :], (2, 512, 77)), 1, 0).astype(jnp.int32)
        _g = jax.random.normal(jax.random.fold_in(_rk, 9001), (2, 1), jnp.float32)
        _g = jnp.sign(_g) * jnp.maximum(jnp.abs(_g), 1.0) + (_g == 0) * 1.0
        g_xattn = _g[0]
        g_ffn = _g[1]
        return (x, ctx_1024, fside_BxSxS2_0, mask_BxSxS2_ik1, g_xattn, g_ffn)
    x, ctx_1024, fside_BxSxS2_0, mask_BxSxS2_ik1, g_xattn, g_ffn = _rec_inputs()

    def _L0_xattn_setup():
        import jax, jax.numpy as jnp
        import numpy as np
        NUM_HEADS = 16
        HIDDEN = 128
        B, S = (2, 256)

        def _split_heads(x, H):
            b, s, d = x.shape
            return x.reshape(b, s, H, d // H).transpose(0, 2, 1, 3)
        key = jax.random.key(seed)
        ks = jax.random.split(key, 14)
        D = HIDDEN
        scale = 1.0 / np.sqrt(D)
        inp = {'query': jax.random.normal(ks[0], (B, S, D), jnp.float32), 'key_in': jax.random.normal(ks[1], (B, S, D), jnp.float32), 'value': jax.random.normal(ks[2], (B, S, D), jnp.float32), 'group_prob': jax.random.uniform(ks[3], (B, S, S), jnp.float32), 'mask': jax.random.randint(ks[4], (B, S, S), 0, 2, jnp.int32), 'wq_k': jax.random.normal(ks[5], (D, D), jnp.float32) * scale, 'wq_b': jnp.zeros((D,), jnp.float32), 'wk_k': jax.random.normal(ks[6], (D, D), jnp.float32) * scale, 'wk_b': jnp.zeros((D,), jnp.float32), 'wv_k': jax.random.normal(ks[7], (D, D), jnp.float32) * scale, 'wv_b': jnp.zeros((D,), jnp.float32), 'wo_k': jax.random.normal(ks[8], (D, D), jnp.float32) * scale, 'wo_b': jnp.zeros((D,), jnp.float32)}
        return inp
    _L0_xattn_all = _L0_xattn_setup()
    _L0_xattn_in = {k: v for k, v in _L0_xattn_all.items() if k in ('wq_k', 'wq_b', 'wk_k', 'wk_b', 'wv_k', 'wv_b', 'wo_k', 'wo_b')}
    del _L0_xattn_all

    def _L0_ffn_setup():
        import jax, jax.numpy as jnp
        import numpy as np
        B, S, D, F, E, K = (4, 256, 128, 512, 8, 2)
        FS = 128
        LN_EPS = 1e-05

        def _swiglu(x, gu_w, dn_w):
            gate, up = jnp.split(x @ gu_w, 2, axis=-1)
            gate = jnp.clip(gate, -10.0, 10.0)
            return jax.nn.silu(gate) * up @ dn_w
        key = jax.random.key(seed)
        ks = jax.random.split(key, 6)
        s = 0.02
        return {'x': jax.random.normal(ks[0], (B, S, D), jnp.float32), 'ln_gamma': jnp.ones((D,), jnp.float32), 'ln_beta': jnp.zeros((D,), jnp.float32), 'router_w': jax.random.normal(ks[1], (D, E), jnp.float32) * s, 'gate_up_w': jax.random.normal(ks[2], (E, D, 2 * F), jnp.float32) * s, 'down_w': jax.random.normal(ks[3], (E, F, D), jnp.float32) * s, 'shared_gate_up_w': jax.random.normal(ks[4], (D, 2 * FS), jnp.float32) * s, 'shared_down_w': jax.random.normal(ks[5], (FS, D), jnp.float32) * s}
    _L0_ffn_all = _L0_ffn_setup()
    _L0_ffn_in = {k: v for k, v in _L0_ffn_all.items() if k in ('ln_gamma', 'ln_beta', 'router_w', 'gate_up_w', 'down_w', 'shared_gate_up_w', 'shared_down_w')}
    del _L0_ffn_all
    return {'x': x, 'ctx_1024': ctx_1024, 'fside_BxSxS2_0': fside_BxSxS2_0, 'mask_BxSxS2_ik1': mask_BxSxS2_ik1, 'g_xattn': g_xattn, 'g_ffn': g_ffn, 'L0_xattn_wq_k': _L0_xattn_in['wq_k'], 'L0_xattn_wq_b': _L0_xattn_in['wq_b'], 'L0_xattn_wk_k': _L0_xattn_in['wk_k'], 'L0_xattn_wk_b': _L0_xattn_in['wk_b'], 'L0_xattn_wv_k': _L0_xattn_in['wv_k'], 'L0_xattn_wv_b': _L0_xattn_in['wv_b'], 'L0_xattn_wo_k': _L0_xattn_in['wo_k'], 'L0_xattn_wo_b': _L0_xattn_in['wo_b'], 'L0_ffn_ln_gamma': _L0_ffn_in['ln_gamma'], 'L0_ffn_ln_beta': _L0_ffn_in['ln_beta'], 'L0_ffn_router_w': _L0_ffn_in['router_w'], 'L0_ffn_gate_up_w': _L0_ffn_in['gate_up_w'], 'L0_ffn_down_w': _L0_ffn_in['down_w'], 'L0_ffn_shared_gate_up_w': _L0_ffn_in['shared_gate_up_w'], 'L0_ffn_shared_down_w': _L0_ffn_in['shared_down_w']}

def reference(x, ctx_1024, fside_BxSxS2_0, mask_BxSxS2_ik1, g_xattn, g_ffn, L0_xattn_wq_k, L0_xattn_wq_b, L0_xattn_wk_k, L0_xattn_wk_b, L0_xattn_wv_k, L0_xattn_wv_b, L0_xattn_wo_k, L0_xattn_wo_b, L0_ffn_ln_gamma, L0_ffn_ln_beta, L0_ffn_router_w, L0_ffn_gate_up_w, L0_ffn_down_w, L0_ffn_shared_gate_up_w, L0_ffn_shared_down_w):
    import jax
    import jax.numpy as jnp

    def _L0_xattn_ref(query, key_in, value, group_prob, mask, wq_k, wq_b, wk_k, wk_b, wv_k, wv_b, wo_k, wo_b):
        import jax, jax.numpy as jnp
        import numpy as np
        NUM_HEADS = 16
        HIDDEN = 128
        B, S = (2, 256)

        def _split_heads(x, H):
            b, s, d = x.shape
            return x.reshape(b, s, H, d // H).transpose(0, 2, 1, 3)
        H = NUM_HEADS
        dh = query.shape[-1] // H
        q = _split_heads(query @ wq_k + wq_b, H)
        k = _split_heads(key_in @ wk_k + wk_b, H)
        v = _split_heads(value @ wv_k + wv_b, H)
        logits = jnp.einsum('bhqd,bhkd->bhqk', q, k) / jnp.sqrt(jnp.asarray(dh, q.dtype))
        neg = (1.0 - mask.astype(q.dtype)) * -1000000000.0
        logits = logits + neg[:, None, :, :]
        attn = jax.nn.softmax(logits, axis=-1)
        attn = attn * group_prob[:, None, :, :]
        out = jnp.einsum('bhqk,bhkd->bhqd', attn, v)
        out = out.transpose(0, 2, 1, 3).reshape(query.shape[0], -1, H * dh)
        return out @ wo_k + wo_b

    def _L0_ffn_ref(x, ln_gamma, ln_beta, router_w, gate_up_w, down_w, shared_gate_up_w, shared_down_w):
        import jax, jax.numpy as jnp
        import numpy as np
        B, S, D, F, E, K = (4, 256, 128, 512, 8, 2)
        FS = 128
        LN_EPS = 1e-05

        def _swiglu(x, gu_w, dn_w):
            gate, up = jnp.split(x @ gu_w, 2, axis=-1)
            gate = jnp.clip(gate, -10.0, 10.0)
            return jax.nn.silu(gate) * up @ dn_w
        b, s, d = x.shape
        xf = x.reshape(-1, d)
        mu = jnp.mean(xf, axis=-1, keepdims=True)
        var = jnp.var(xf, axis=-1, keepdims=True)
        xn = (xf - mu) * jax.lax.rsqrt(var + LN_EPS) * ln_gamma + ln_beta
        logits = xn @ router_w
        probs = jax.nn.softmax(logits, axis=-1)
        topv, topi = jax.lax.top_k(probs, K)
        topv = topv / jnp.sum(topv, axis=-1, keepdims=True)
        comb = jnp.sum(jax.nn.one_hot(topi, E, dtype=xn.dtype) * topv[..., None], axis=1)
        out = jnp.zeros_like(xf)
        for e in range(E):
            out = out + comb[:, e:e + 1] * _swiglu(xn, gate_up_w[e], down_w[e])
        out = out + _swiglu(xn, shared_gate_up_w, shared_down_w)
        return out.reshape(b, s, d)
    x = x + jnp.tanh(g_xattn[0]) * _L0_xattn_ref(_layernorm(x, axis=-1), ctx_1024, ctx_1024, fside_BxSxS2_0, mask_BxSxS2_ik1, L0_xattn_wq_k, L0_xattn_wq_b, L0_xattn_wk_k, L0_xattn_wk_b, L0_xattn_wv_k, L0_xattn_wv_b, L0_xattn_wo_k, L0_xattn_wo_b)
    x = x + jnp.tanh(g_ffn[0]) * _L0_ffn_ref(_layernorm(x, axis=-1), L0_ffn_ln_gamma, L0_ffn_ln_beta, L0_ffn_router_w, L0_ffn_gate_up_w, L0_ffn_down_w, L0_ffn_shared_gate_up_w, L0_ffn_shared_down_w)
    return x

_drawn_inputs = setup_inputs


def setup_inputs(seed=0):
    import zlib

    import numpy as np

    out = dict(_drawn_inputs(seed))
    spreads = {'L0_xattn_wq_b': (0.0, 0.8),
     'L0_xattn_wk_b': (0.0, 0.8),
     'L0_xattn_wv_b': (0.0, 0.1),
     'L0_xattn_wo_b': (0.0, 0.1),
     'L0_ffn_ln_gamma': (1.0, 0.6),
     'L0_ffn_ln_beta': (0.0, 0.8)}
    factors = {'L0_ffn_router_w': 7.859,
     'L0_ffn_gate_up_w': 6.846,
     'L0_ffn_down_w': 6.869,
     'L0_ffn_shared_gate_up_w': 8.0,
     'L0_ffn_shared_down_w': 8.0}
    for name, (base, spread) in spreads.items():
        noise = np.random.default_rng([zlib.crc32(name.encode()), seed]).standard_normal(out[name].shape)
        drawn = base * np.exp(spread * noise) if base else spread * noise
        out[name] = jnp.asarray(drawn.astype(out[name].dtype))
    for name, factor in factors.items():
        out[name] = (out[name] * factor).astype(out[name].dtype)
    return out
```

```python
from contextlib import ExitStack

import concourse.bass as bass
from concourse import mybir

ALU = mybir.AluOpType
ACT = mybir.ActivationFunctionType
F32 = mybir.dt.float32
F32R = mybir.dt.float32r
BF16 = mybir.dt.bfloat16
I32 = mybir.dt.int32
U32 = mybir.dt.uint32
AX_X = mybir.AxisListType.X


def gated_block(nc, x, ctx_in, group_prob, mask, g_xattn, g_ffn, wq, bq, wk, bk, wv, bv, wo, bo,
                ln_gamma, ln_beta, router_w, gate_up_w, down_w, sh_gate_up_w, sh_down_w, out):
    P = 128
    B, S, D = x.shape
    S2 = ctx_in.shape[1]
    KP = S2 + S2 % 2
    H, DH = 16, D // 16
    G = 4
    HG = H // G
    TPB = S // P
    NT = B * TPB
    TOK = B * S
    E, F = down_w.shape[0], down_w.shape[1]
    FS = sh_down_w.shape[0]
    FC = F // P
    TOPK = 2
    PAIRS = TOPK * NT
    SLOT_TILES = TOK * TOPK // P + E - 1
    JC = SLOT_TILES + SLOT_TILES % 2
    EPS = 1e-5
    QSCALE = float(DH) ** -0.5
    assert D == P and FS == P and H == G * HG and HG * KP <= 512

    x_tiles = x.rearrange("b (t p) d -> p (b t) d", p=P)
    gp_tiles = group_prob.rearrange("b (t p) k -> p (b t) k", p=P)
    mask_tiles = mask.rearrange("b (t p) k -> p (b t) k", p=P)
    out_tiles = out.rearrange("b (t p) d -> p (b t) d", p=P)
    normed_dram = nc.dram_tensor("normed_rows", (TOK, D), F32, kind="Internal").ap()
    chosen_dram = nc.dram_tensor("chosen_rows", (TOPK * TOK + SLOT_TILES * P, D), F32, kind="Internal").ap()

    with ExitStack() as ctx:
        def sb(name, shape, dt=F32):
            return ctx.enter_context(nc.sbuf_tensor(name, shape, dt))

        def sem(name):
            return ctx.enter_context(nc.semaphore(name))

        bank = [ctx.enter_context(nc.psum_tensor(f"bank{i}", [P, 512], F32)) for i in range(8)]

        x_sb = sb("x_sb", [P, NT, D])
        ctx_sb = sb("ctx_sb", [S2, B, D])
        gp_sb = sb("gp_sb", [P, NT, S2])
        mask_sb = sb("mask_sb", [P, NT, S2], I32)
        wq_sb, wk_sb, wv_sb, wo_sb = (sb(n, [P, D]) for n in ("wq_sb", "wk_sb", "wv_sb", "wo_sb"))
        col_sb = sb("col_sb", [P, 4])
        bv_sb = sb("bv_sb", [S2, D])
        bo_sb = sb("bo_sb", [P, D])
        gates_sb = sb("gates_sb", [P, 2])
        router_sb = sb("router_sb", [P, E])
        gu_sb = sb("gu_sb", [P, E * 2 * F])
        down_sb = sb("down_sb", [P, E * FC * D])
        shgu_sb = sb("shgu_sb", [P, 2 * FS])
        shdown_sb = sb("shdown_sb", [P, D])

        ident = sb("ident", [P, P])
        ident_r = sb("ident_r", [P, P], F32R)
        earlier = sb("earlier", [P, P], BF16)
        ones = sb("ones", [P, P], BF16)
        upto = sb("upto", [P, E, E])
        part_i = sb("part_i", [P, HG], I32)
        part_b = sb("part_b", [P, HG], I32)
        part_c = sb("part_c", [P, HG], I32)
        headsel = sb("headsel", [P, HG])
        iota_i = sb("iota_i", [P, P], I32)
        iota_f = sb("iota_f", [P, P])
        tok_i = sb("tok_i", [P, PAIRS], I32)
        tok_f = sb("tok_f", [P, PAIRS])
        row_i = sb("row_i", [P, PAIRS], I32)
        row_f = sb("row_f", [P, PAIRS])
        dump_i = sb("dump_i", [P, JC], I32)
        dump_f = sb("dump_f", [P, JC])
        neghalf = sb("neghalf", [P, NT])

        stats = sb("stats", [P, NT, 6])
        meanvar = sb("meanvar", [P, NT, 2])
        veps = sb("veps", [P, NT])
        rstd = sb("rstd", [P, NT])
        z_sb = sb("z_sb", [P, NT, D])
        zT = sb("zT", [P, TOK])
        qT = sb("qT", [P, TOK])
        bq_scaled = sb("bq_scaled", [P, 1])
        ctxT = sb("ctxT", [P, B, S2])
        kT = sb("kT", [P, B, S2])
        kblock = sb("kblock", [P, B, HG, KP])
        v_pad = sb("v_pad", [S2, B, G, HG, HG, DH])
        neg = sb("neg", [P, NT, S2])
        neg_hi = sb("neg_hi", [P, NT, KP], F32R)
        neg_lo = sb("neg_lo", [P, NT, KP], F32R)
        tanh_g = sb("tanh_g", [P, 2])
        xb = sb("xb", [P, NT, D])
        top = sb("top", [P, 2, H])
        shifted = sb("shifted", [P, 2, H, S2])
        expd = sb("expd", [P, 2, H, S2])
        prob = sb("prob", [P, 2, H, S2])
        probT = sb("probT", [P, 2, HG, G, P])
        sums = sb("sums", [P, 2, H])
        rsum = sb("rsum", [P, 2, H])
        rsum_wide = sb("rsum_wide", [P, 2, H, DH])
        rsumT = sb("rsumT", [P, 2, P])
        attT = sb("attT", [P, 2, P])
        x1 = sb("x1", [P, NT, D])

        stats2 = sb("stats2", [P, NT, 6])
        meanvar2 = sb("meanvar2", [P, NT, 2])
        veps2 = sb("veps2", [P, NT])
        rstd2 = sb("rstd2", [P, NT])
        veps3 = sb("veps3", [P, NT])
        rstd3 = sb("rstd3", [P, NT])
        rr = sb("rr", [P, NT])
        z2 = z_sb
        x2T = zT
        logit = sb("logit", [P, NT, E])
        best = sb("best", [P, NT, 8])
        best_i = sb("best_i", [P, NT, 8], U32)
        choice_f = sb("choice_f", [P, TOPK, NT])
        onehot = sb("onehot", [P, TOPK, NT, E])
        member = sb("member", [P, NT, E], BF16)
        gap = sb("gap", [P, NT])
        egap = sb("egap", [P, NT])
        egap1 = sb("egap1", [P, NT])
        wgt = sb("wgt", [P, TOPK, NT])
        wgt_g = sb("wgt_g", [P, TOPK, NT])
        cnt_i = sb("cnt_i", [P, E], I32)
        tiles_i = sb("tiles_i", [P, E], I32)
        tiles_f = sb("tiles_f", [P, E])
        tiles_sq = sb("tiles_sq", [P, E, E])
        tiles_incl = sb("tiles_incl", [P, E])
        tiles_excl = sb("tiles_excl", [P, E])
        start = sb("start", [P, E])
        slot_te = sb("slot_te", [P, NT, E])
        slot_sel = sb("slot_sel", [P, TOPK, NT, E])
        slot_f = sb("slot_f", [P, PAIRS])
        slot_i = sb("slot_i", [P, PAIRS], I32)
        sj_i = sb("sj_i", [P, PAIRS], I32)
        sr_i = sb("sr_i", [P, PAIRS], I32)
        sj_f = sb("sj_f", [P, PAIRS])
        sr_f = sb("sr_f", [P, PAIRS])
        hot_r = probT[:, 0].rearrange("p i g q -> p (i g) q")
        hot_j = sb("hot_j", [P, PAIRS, JC])
        vals = sb("vals", [P, PAIRS, 3])
        hot_v = sb("hot_v", [P, PAIRS, 3, JC])
        gidx = sb("gidx", [P, JC], I32)
        sidx = sb("sidx", [P, JC], I32)
        wslot = sb("wslot", [P, JC])
        past = sb("past", [P, JC, E])
        exp_f = sb("exp_f", [P, JC])
        exp_c = sb("exp_c", [P, JC])
        exp_i = sb("exp_i", [P, JC], I32)

        sh_gate = sb("sh_gate", [P, TOK])
        sh_silu = qT
        sh_hT = sb("sh_hT", [P, TOK])
        base = sb("base", [P, NT, D])

        xg = sb("xg", [P, 2, D])
        xgT = sb("xgT", [P, 2, P])
        gate = sb("gate", [P, 2, F])
        silu = sb("silu", [P, 2, F])
        hid = sb("hid", [P, 2, F])
        hidT = sb("hidT", [P, 2, F])
        y_all = sb("y_all", [P, SLOT_TILES, D])
        chosen = hot_r.rearrange("p (k t) d -> p k t d", k=TOPK)
        sum1 = xb
        result = x_sb

        names = """x_in0 x_in1 ctx_in kv_in q_in col_in gp_in mask_in small_in sh_in gate_in
            w_in const iota_s headsel_s ident_s identr_s
            stats_s mv_s veps_s rstd_s z_s zT_ps zT_sb q_ps qT_s bqs_s
            ctxT_ps ctxT_sb k_ps kT_s kb_s kz_s v_ps vz_s v_s neg_s negz_s neghi_s neglo_s tanh_s xb_s
            score_s max_s shift_s exp_s prob_s pt_ps pt_sb o_ps r_ps r_sb sum_s rsum_s rwide_s
            att_s y_ps x1_s st2_s mv2_s ve2_s rs2_s ve3_s rs3_s rr_s z2_s z2_out x2_ps x2_s
            log_ps dstep gap_s egap_s member_s rank_ps cnt_ps vals_s list_ps list_s expert_s
            shg_ps shc_s shsilu_s shh_s shd_ps base_s
            xg_s0 xg_s1 xgT_ps xgT_s gu_ps clip_s silu_s hid_s hT_ps hT_s yy_ps yy_s
            scat_s chosen_s sum1_s result_s out_s""".split()
        s = {n: sem(n) for n in names}

        block = ctx.enter_context(nc.Block())

        @block.sync
        def _(sp):
            sp.dma_start(x_sb[:, 0:TPB, :], x_tiles[:, 0:TPB, :]).then_inc(s["x_in0"], 16)
            sp.dma_start(wq_sb[:], wq).then_inc(s["q_in"], 16)
            sp.dma_start(x_sb[:, TPB:NT, :], x_tiles[:, TPB:NT, :]).then_inc(s["x_in1"], 16)
            sp.dma_start(gp_sb[:], gp_tiles).then_inc(s["gp_in"], 16)
            sp.dma_start(wo_sb[:], wo).then_inc(s["small_in"], 16)
            sp.dma_start(router_sb[:], router_w).then_inc(s["small_in"], 16)
            sp.dma_start(shgu_sb[:], sh_gate_up_w).then_inc(s["sh_in"], 16)
            sp.dma_start(shdown_sb[:], sh_down_w).then_inc(s["sh_in"], 16)
            for e in range(E):
                sp.dma_start(gu_sb[:, e * 2 * F:(e + 1) * 2 * F], gate_up_w[e]).then_inc(s["w_in"], 16)
                sp.dma_start(down_sb[:, e * FC * D:(e + 1) * FC * D].rearrange("p (c d) -> p c d", c=FC),
                             down_w[e].rearrange("(c p) d -> p c d", p=P)).then_inc(s["w_in"], 16)
            sp.wait_ge(s["z2_s"], NT)
            sp.dma_start(normed_dram.rearrange("(t p) d -> p t d", p=P), z2[:]).then_inc(s["z2_out"], 16)
            sp.wait_ge(s["scat_s"], 16 * SLOT_TILES)
            sp.dma_start(chosen, chosen_dram[0:TOPK * TOK, :].rearrange("(k t p) d -> p k t d", k=TOPK, p=P))\
                .then_inc(s["chosen_s"], 16)
            sp.wait_ge(s["result_s"], 1)
            sp.dma_start(out_tiles, result[:]).then_inc(s["out_s"], 16)
            sp.wait_ge(s["out_s"], 16)

        @block.gpsimd
        def _(pool):
            pool.memset(neghalf[:], -0.5).then_inc(s["const"], 1)
            pool.memset(ident[:], 0.0).then_inc(s["const"], 1)
            pool.wait_ge(s["const"], 2)
            pool.affine_select(out=ident[:], in_=ident[:], compare_op=ALU.not_equal, fill=1.0, base=0,
                               pattern=[[-1, P]], channel_multiplier=1).then_inc(s["ident_s"], 1)
            pool.iota(part_i[:], [[0, HG]], base=0, channel_multiplier=1).then_inc(s["iota_s"], 1)
            pool.iota(iota_i[:], [[1, P]], base=0, channel_multiplier=0).then_inc(s["iota_s"], 1)
            pool.wait_ge(s["veps_s"], 1)
            pool.tensor_tensor(rstd[:], veps[:], neghalf[:], ALU.pow).then_inc(s["rstd_s"], 1)
            pool.memset(v_pad[:], 0.0).then_inc(s["vz_s"], 1)
            pool.memset(kblock[:], 0.0).then_inc(s["kz_s"], 1)
            pool.iota(tok_i[:], [[0, TOPK], [P, NT]], base=0, channel_multiplier=1).then_inc(s["iota_s"], 1)
            pool.iota(row_i[:], [[TOK, TOPK], [P, NT]], base=0, channel_multiplier=1).then_inc(s["iota_s"], 1)
            pool.iota(dump_i[:], [[P, JC]], base=TOPK * TOK, channel_multiplier=1).then_inc(s["iota_s"], 1)
            pool.memset(ones[:], 1.0).then_inc(s["const"], 1)
            pool.memset(earlier[:], 1.0).then_inc(s["const"], 1)
            pool.memset(upto[:], 1.0).then_inc(s["const"], 1)
            pool.wait_ge(s["const"], 5)
            pool.affine_select(out=earlier[:], in_=earlier[:], compare_op=ALU.is_gt, fill=0.0, base=0,
                               pattern=[[1, P]], channel_multiplier=-1).then_inc(s["const"], 1)
            pool.affine_select(out=upto[:], in_=upto[:], compare_op=ALU.is_ge, fill=0.0, base=0,
                               pattern=[[1, E], [-1, E]], channel_multiplier=0).then_inc(s["const"], 1)
            pool.wait_ge(s["gp_in"], 16)
            for t in range(NT):
                u = t % 2
                pool.wait_ge(s["exp_s"], t + 1)
                if t >= 2:
                    pool.wait_ge(s["pt_ps"], HG * (t - 1))
                pool.tensor_tensor(prob[:, u], expd[:, u], gp_sb[:, t:t + 1, :].to_broadcast([P, H, S2]),
                                   ALU.mult).then_inc(s["prob_s"], 1)
            pool.wait_ge(s["ve2_s"], 1)
            pool.tensor_tensor(rstd2[:], veps2[:], neghalf[:], ALU.pow).then_inc(s["rs2_s"], 1)
            pool.wait_ge(s["ve3_s"], 1)
            pool.tensor_tensor(rstd3[:], veps3[:], neghalf[:], ALU.pow).then_inc(s["rs3_s"], 1)

            pool.wait_ge(s["z2_out"], 16)
            pool.wait_ge(s["list_s"], 3)

            def gather(j):
                if j >= 2:
                    pool.wait_ge(s["xgT_ps"], j - 1)
                pool.indirect_dma_start(xg[:, j % 2, :], None, normed_dram,
                                        bass.IndirectOffsetOnAxis(ap=gidx[:, j:j + 1], axis=0))\
                    .then_inc(s[f"xg_s{j % 2}"], 16)

            def scatter(j):
                pool.wait_ge(s["yy_s"], j + 1)
                pool.indirect_dma_start(chosen_dram, bass.IndirectOffsetOnAxis(ap=sidx[:, j:j + 1], axis=0),
                                        y_all[:, j, :], None).then_inc(s["scat_s"], 16)

            for j in range(SLOT_TILES):
                gather(j)
                if j >= 5:
                    scatter(j - 5)
            for j in range(SLOT_TILES - 5, SLOT_TILES):
                scatter(j)

        @block.scalar
        def _(act):
            act.dma_start(ctx_sb[:], ctx_in.rearrange("b k d -> k b d")).then_inc(s["ctx_in"], 16)
            act.dma_start(wk_sb[:], wk).then_inc(s["kv_in"], 16)
            act.dma_start(wv_sb[:], wv).then_inc(s["kv_in"], 16)
            act.dma_start(bv_sb[:], bv.rearrange("(a d) -> a d", a=1).to_broadcast([S2, D])).then_inc(s["kv_in"], 16)
            for n, v in enumerate((bq, bk, ln_gamma, ln_beta)):
                act.dma_start(col_sb[:, n:n + 1], v.rearrange("(d a) -> d a", a=1)).then_inc(s["col_in"], 16)
            act.dma_start(mask_sb[:], mask_tiles).then_inc(s["mask_in"], 16)
            act.dma_start(gates_sb[:, 0:1], g_xattn.rearrange("(a d) -> a d", a=1).to_broadcast([P, 1])).then_inc(s["gate_in"], 16)
            act.dma_start(gates_sb[:, 1:2], g_ffn.rearrange("(a d) -> a d", a=1).to_broadcast([P, 1])).then_inc(s["gate_in"], 16)
            act.dma_start(bo_sb[:], bo.rearrange("(a d) -> a d", a=1).to_broadcast([P, D])).then_inc(s["gate_in"], 16)

            def evac(dst, src):
                return act.activation(dst, src, ACT.Copy)

            act.wait_ge(s["ctxT_ps"], 1)
            evac(ctxT[:], bank[2][:, 0:B * S2].rearrange("p (b k) -> p b k", b=B)).then_inc(s["ctxT_sb"], 1)
            for b in range(B):
                act.wait_ge(s["zT_ps"], b + 1)
                evac(zT[:, b * S:(b + 1) * S], bank[b][:]).then_inc(s["zT_sb"], 1)
                if b == 0:
                    act.wait_ge(s["bqs_s"], 1)
                act.wait_ge(s["q_ps"], b + 1)
                act.activation(qT[:, b * S:(b + 1) * S], bank[4 + b][:], ACT.Identity, bias=bq_scaled[:, 0:1],
                               scale=QSCALE).then_inc(s["qT_s"], 1)
            act.wait_ge(s["gate_in"], 48)
            act.activation(tanh_g[:], gates_sb[:], ACT.Tanh).then_inc(s["tanh_s"], 1)

            def exp_tile(t):
                u = t % 2
                act.wait_ge(s["shift_s"], t + 1)
                if t >= 2:
                    act.wait_ge(s["prob_s"], t - 1)
                    act.wait_ge(s["sum_s"], t - 1)
                act.activation(expd[:, u], shifted[:, u], ACT.Exp).then_inc(s["exp_s"], 1)

            def back_tile(t):
                u = t % 2
                for i in range(HG):
                    act.wait_ge(s["pt_ps"], HG * t + i + 1)
                    if i == 0 and t >= 2:
                        act.wait_ge(s["o_ps"], t - 1)
                    evac(probT[0:S2, u, i], bank[4 + i % 2][0:S2, :].rearrange("p (g q) -> p g q", g=G))\
                        .then_inc(s["pt_sb"], 1)
                act.wait_ge(s["r_ps"], t + 1)
                if t >= 2:
                    act.wait_ge(s["att_s"], t - 1)
                evac(rsumT[:, u], bank[6][:, P:2 * P]).then_inc(s["r_sb"], 1)

            for t in range(NT + 1):
                if t < NT:
                    exp_tile(t)
                if t >= 1:
                    back_tile(t - 1)

            for b in range(B):
                act.wait_ge(s["x2_ps"], b + 1)
                act.activation(x2T[:, b * S:(b + 1) * S], bank[b][:], ACT.Identity, bias=col_sb[:, 3:4],
                               scale=col_sb[:, 2:3]).then_inc(s["x2_s"], 1)
            act.wait_ge(s["gap_s"], 1)
            act.activation(egap[:], gap[:], ACT.Exp).then_inc(s["egap_s"], 1)
            for b in range(B):
                act.wait_ge(s["shc_s"], b + 1)
                act.activation(sh_silu[:, b * S:(b + 1) * S], sh_gate[:, b * S:(b + 1) * S], ACT.Silu)\
                    .then_inc(s["shsilu_s"], 1)

            def silu_tile(j, u):
                act.wait_ge(s["clip_s"], j + 1)
                act.activation(silu[:, u], gate[:, u], ACT.Silu).then_inc(s["silu_s"], 1)

            def hidT_tile(j, u):
                act.wait_ge(s["hT_ps"], j + 1)
                evac(hidT[:, u], bank[6][:]).then_inc(s["hT_s"], 1)

            def y_tile(j, u):
                act.wait_ge(s["yy_ps"], j + 1)
                act.activation(y_all[:, bass.ds(j, 1), :].rearrange("p a d -> p (a d)"), bank[7][:, 0:D],
                               ACT.Copy, scale=wslot[:, bass.ds(j, 1)]).then_inc(s["yy_s"], 1)

            act.wait_ge(s["list_s"], 3)
            silu_tile(0, 0)
            silu_tile(1, 1)
            hidT_tile(0, 0)
            silu_tile(2, 0)
            hidT_tile(1, 1)
            y_tile(0, 0)
            with act.Fori(0, (SLOT_TILES - 3) // 2) as i:
                for v in range(2):
                    j = i * 2 + (3 + v)
                    silu_tile(j, (3 + v) % 2)
                    hidT_tile(i * 2 + (2 + v), v % 2)
                    y_tile(i * 2 + (1 + v), (1 + v) % 2)
            hidT_tile(SLOT_TILES - 1, 0)
            y_tile(SLOT_TILES - 2, 1)
            y_tile(SLOT_TILES - 1, 0)

        @block.tensor
        def _(pe):
            pe.wait_ge(s["ident_s"], 1)
            pe.wait_ge(s["ctx_in"], 16)
            for b in range(B):
                m = pe.transpose(bank[2][:, b * S2:(b + 1) * S2], ctx_sb[:, b, :], ident[0:S2, 0:S2])
            m.then_inc(s["ctxT_ps"], 1)
            pe.wait_ge(s["ctxT_sb"], 1)
            pe.wait_ge(s["kv_in"], 48)
            pe.matmul(bank[3][:, 0:B * S2], wk_sb[:], ctxT[:].rearrange("p b k -> p (b k)"), start=True, stop=True)\
                .then_inc(s["k_ps"], 1)
            for b in range(B):
                m = pe.matmul(bank[6 + b][0:S2, 0:D], ctxT[:, b, :], wv_sb[:], start=True, stop=True)
            m.then_inc(s["v_ps"], 1)
            for b in range(B):
                pe.wait_ge(s["z_s"], TPB * (b + 1))
                for t in range(TPB):
                    m = pe.transpose(bank[b][:, t * P:(t + 1) * P], z_sb[:, b * TPB + t, :], ident[:])
                m.then_inc(s["zT_ps"], 1)
            for b in range(B):
                pe.wait_ge(s["zT_sb"], b + 1)
                if b == 0:
                    pe.wait_ge(s["q_in"], 16)
                pe.matmul(bank[4 + b][:], wq_sb[:], zT[:, b * S:(b + 1) * S], start=True, stop=True)\
                    .then_inc(s["q_ps"], 1)

            def scores(t):
                b = t // TPB
                if t == 0:
                    pe.wait_ge(s["identr_s"], 1)
                    pe.wait_ge(s["neglo_s"], 1)
                    pe.wait_ge(s["neghi_s"], 1)
                    pe.wait_ge(s["negz_s"], 2)
                    pe.wait_ge(s["zT_sb"], B)
                    pe.wait_ge(s["kT_s"], 1)
                    pe.wait_ge(s["kb_s"], B)
                if t % TPB == 0:
                    pe.wait_ge(s["qT_s"], b + 1)
                if t >= 1:
                    pe.wait_ge(s["shift_s"], t)
                for g in range(G):
                    dst = bank[g][:, 0:HG * KP]
                    for n, part in enumerate((neg_hi, neg_lo)):
                        pe.matmul(dst, ident_r[:], part[:, t:t + 1, :].to_broadcast([P, HG, KP]),
                                  start=(n == 0), stop=False)
                for g in range(G):
                    r = slice(32 * g, 32 * g + 32)
                    m = pe.matmul(bank[g][:, 0:HG * KP], qT[r, t * P:(t + 1) * P],
                                  kblock[r, b].rearrange("p i k -> p (i k)"), start=False, stop=True)
                m.then_inc(s["score_s"], 1)

            def attend(t):
                b, u = t // TPB, t % 2
                pe.wait_ge(s["prob_s"], t + 1)
                if t == 0:
                    pe.wait_ge(s["qT_s"], B)
                    pe.wait_ge(s["v_s"], B * HG)

                def turn(i):
                    k = HG * t + i
                    if k >= 2:
                        pe.wait_ge(s["pt_sb"], k - 1)
                    for g in range(G):
                        m = pe.transpose(bank[4 + i % 2][0:S2, g * P:(g + 1) * P], prob[:, u, G * g + i, :], ident[:])
                    m.then_inc(s["pt_ps"], 1)

                def weigh(i):
                    pe.wait_ge(s["pt_sb"], HG * t + i + 1)
                    if i == 0 and t >= 1:
                        pe.wait_ge(s["att_s"], t)
                    for g in range(G):
                        m = pe.matmul(bank[6][32 * g:32 * g + 32, 0:P],
                                      v_pad[:, b, g, i].rearrange("p a d -> p (a d)"), probT[0:S2, u, i, g, :],
                                      start=(i == 0), stop=(i == HG - 1))
                    return m

                turn(0)
                turn(1)
                for i in range(HG):
                    m = weigh(i)
                    if i + 2 < HG:
                        turn(i + 2)
                m.then_inc(s["o_ps"], 1)
                pe.wait_ge(s["rwide_s"], t + 1)
                pe.transpose(bank[6][:, P:2 * P], rsum_wide[:, u].rearrange("p h d -> p (h d)"), ident[:])\
                    .then_inc(s["r_ps"], 1)

            def project(t):
                pe.wait_ge(s["att_s"], t + 1)
                if t == 0:
                    pe.wait_ge(s["small_in"], 32)
                else:
                    pe.wait_ge(s["x1_s"], t)
                pe.matmul(bank[7][:, 0:D], attT[:, t % 2], wo_sb[:], start=True, stop=True).then_inc(s["y_ps"], 1)

            for t in range(NT + 3):
                if t < NT:
                    scores(t)
                if 2 <= t < NT + 2:
                    attend(t - 2)
                if t >= 3:
                    project(t - 3)

            for b in range(B):
                pe.wait_ge(s["z2_s"], TPB * (b + 1))
                for t in range(TPB):
                    m = pe.transpose(bank[b][:, t * P:(t + 1) * P], z2[:, b * TPB + t, :], ident[:])
                m.then_inc(s["x2_ps"], 1)
            for t in range(NT):
                if t % TPB == 0:
                    pe.wait_ge(s["x2_s"], t // TPB + 1)
                m = pe.matmul(bank[2][:, t * E:(t + 1) * E], x2T[:, t * P:(t + 1) * P], router_sb[:],
                              start=True, stop=True)
            m.then_inc(s["log_ps"], 1)
            pe.wait_ge(s["sh_in"], 32)
            pe.wait_ge(s["x2_s"], B)
            for b in range(B):
                pe.matmul(bank[b][:], shgu_sb[:, 0:FS], x2T[:, b * S:(b + 1) * S], start=True, stop=True)
                pe.matmul(bank[4 + b][:], shgu_sb[:, FS:2 * FS], x2T[:, b * S:(b + 1) * S], start=True, stop=True)\
                    .then_inc(s["shg_ps"], 1)
            pe.wait_ge(s["member_s"], 1)
            rank = bank[3][:, 0:NT * E]
            for t in range(NT - 1):
                n = NT - 1 - t
                pe.matmul(bank[3][:, (t + 1) * E:NT * E], ones[:], member[:, t:t + 1, :].to_broadcast([P, n, E]),
                          start=(t == 0), stop=False, skip_group_check=True)
            m = pe.matmul(rank, earlier[:], member[:].rearrange("p t e -> p (t e)"), start=False, stop=True,
                          skip_group_check=True)
            m.then_inc(s["rank_ps"], 1)
            for t in range(NT):
                m = pe.matmul(bank[6][:, 0:E], ones[:], member[:, t, :], start=(t == 0), stop=(t == NT - 1))
            m.then_inc(s["cnt_ps"], 1)
            pe.wait_ge(s["vals_s"], 1)
            for n in range(PAIRS):
                m = pe.matmul(bank[7][:, 0:3 * JC], hot_r[:, n, :], hot_v[:, n].rearrange("p v j -> p (v j)"),
                              start=(n == 0), stop=(n == PAIRS - 1))
            m.then_inc(s["list_ps"], 1)

            for b in range(B):
                pe.wait_ge(s["shh_s"], b + 1)
                for t in range(TPB):
                    m = pe.matmul(bank[b][:, t * D:(t + 1) * D], sh_hT[:, (b * TPB + t) * P:(b * TPB + t + 1) * P],
                                  shdown_sb[:], start=True, stop=True)
                m.then_inc(s["shd_ps"], 1)

            def rows_tile(j, u, nth):
                pe.wait_ge(s[f"xg_s{u}"], nth * 16)
                if not isinstance(j, int) or j > 0:
                    pe.wait_ge(s["xgT_s"], j)
                pe.transpose(bank[0][:, 0:P], xg[:, u], ident[:]).then_inc(s["xgT_ps"], 1)

            def gate_up_tile(j, u):
                e = pe.value_load(exp_i[0:1, bass.ds(j, 1)], min_val=0, max_val=E - 1)
                pe.wait_ge(s["xgT_s"], j + 1)
                if not isinstance(j, int) or j > 1:
                    pe.wait_ge(s["hid_s"], j - 1)
                pe.matmul(bank[2 + u][:], xgT[:, u], gu_sb[:, bass.ds(e * (2 * F), F)], start=True, stop=True)\
                    .then_inc(s["gu_ps"], 1)
                pe.matmul(bank[4 + u][:], xgT[:, u], gu_sb[:, bass.ds(e * (2 * F) + F, F)], start=True, stop=True)\
                    .then_inc(s["gu_ps"], 1)

            def hidden_tile(j, u):
                pe.wait_ge(s["hid_s"], j + 1)
                if not isinstance(j, int) or j > 0:
                    pe.wait_ge(s["hT_s"], j)
                for c in range(FC):
                    m = pe.transpose(bank[6][:, c * P:(c + 1) * P], hid[:, u, c * P:(c + 1) * P], ident[:])
                m.then_inc(s["hT_ps"], 1)

            def down_tile(j, u):
                e = pe.value_load(exp_i[0:1, bass.ds(j, 1)], min_val=0, max_val=E - 1)
                pe.wait_ge(s["hT_s"], j + 1)
                if not isinstance(j, int) or j > 0:
                    pe.wait_ge(s["yy_s"], j)
                for c in range(FC):
                    m = pe.matmul(bank[7][:, 0:D], hidT[:, u, c * P:(c + 1) * P],
                                  down_sb[:, bass.ds(e * (FC * D) + c * D, D)], start=(c == 0), stop=(c == FC - 1))
                m.then_inc(s["yy_ps"], 1)

            pe.wait_ge(s["w_in"], 16 * 2 * E)
            pe.wait_ge(s["expert_s"], 1)
            pe.wait_ge(s["base_s"], NT)
            pe.wait_ge(s["list_s"], 3)
            rows_tile(0, 0, 1)
            rows_tile(1, 1, 1)
            gate_up_tile(0, 0)
            rows_tile(2, 0, 2)
            gate_up_tile(1, 1)
            hidden_tile(0, 0)
            rows_tile(3, 1, 2)
            gate_up_tile(2, 0)
            hidden_tile(1, 1)
            down_tile(0, 0)
            with pe.Fori(0, (SLOT_TILES - 5) // 2) as i:
                for v in range(2):
                    rows_tile(i * 2 + (4 + v), v % 2, i + 3)
                    gate_up_tile(i * 2 + (3 + v), (3 + v) % 2)
                    hidden_tile(i * 2 + (2 + v), v % 2)
                    down_tile(i * 2 + (1 + v), (1 + v) % 2)
            for j in range(SLOT_TILES - 2, SLOT_TILES + 2):
                if j + 1 < SLOT_TILES:
                    rows_tile(j + 1, (j + 1) % 2, (j + 1) // 2 + 1)
                if j < SLOT_TILES:
                    gate_up_tile(j, j % 2)
                if j - 1 < SLOT_TILES:
                    hidden_tile(j - 1, (j - 1) % 2)
                down_tile(j - 2, j % 2)

        @block.vector
        def _(dve):
            steps = [0]

            def step(ins):
                steps[0] += 1
                ins.then_inc(s["dstep"], 1)
                dve.wait_ge(s["dstep"], steps[0])

            def layer_stats(b, src, st, mv, name_st):
                for t in range(b * TPB, (b + 1) * TPB):
                    dve.bn_stats(st[:, t, :], src[:, t, :]).then_inc(s[name_st], 1)
                for t in range(b * TPB, (b + 1) * TPB):
                    dve.wait_ge(s[name_st], t + 1)
                    dve.bn_aggr(mv[:, t, :], st[:, t, :]).then_inc(s["mv_s"], 1)

            for b in range(B):
                dve.wait_ge(s[f"x_in{b}"], 16)
                layer_stats(b, x_sb, stats, meanvar, "stats_s")
            dve.wait_ge(s["mv_s"], NT)
            dve.tensor_scalar(veps[:], meanvar[:, :, 1], EPS, None, ALU.add).then_inc(s["veps_s"], 1)
            dve.wait_ge(s["col_in"], 64)
            dve.tensor_scalar(bq_scaled[:], col_sb[:, 0:1], QSCALE, None, ALU.mult).then_inc(s["bqs_s"], 1)
            dve.memset(neg_hi[:, :, S2:KP].bitcast(F32), 0.0).then_inc(s["negz_s"], 1)
            dve.memset(neg_lo[:, :, S2:KP].bitcast(F32), 0.0).then_inc(s["negz_s"], 1)
            dve.wait_ge(s["mask_in"], 16)
            step(dve.tensor_scalar(neg[:], mask_sb[:], -1.0, 1e9, ALU.add, ALU.mult))
            dve.tensor_copy(neg_hi[:, :, 0:S2], neg[:]).then_inc(s["neghi_s"], 1)
            dve.wait_ge(s["neghi_s"], 1)
            dve.tensor_tensor(neg_lo[:, :, 0:S2], neg[:], neg_hi[:, :, 0:S2].bitcast(F32), ALU.subtract)\
                .then_inc(s["neglo_s"], 1)
            dve.wait_ge(s["ident_s"], 1)
            dve.tensor_copy(ident_r[:], ident[:]).then_inc(s["identr_s"], 1)
            dve.wait_ge(s["rstd_s"], 1)
            for t in range(NT):
                dve.tensor_scalar(z_sb[:, t, :], x_sb[:, t, :], meanvar[:, t, 0:1], rstd[:, t:t + 1],
                                  ALU.subtract, ALU.mult).then_inc(s["z_s"], 1)
            dve.wait_ge(s["iota_s"], 2)
            step(dve.tensor_scalar(part_b[:], part_i[:], 3, HG - 1, ALU.logical_shift_right, ALU.bitwise_and))
            step(dve.tensor_copy(part_c[:], iota_i[:, 0:HG]))
            step(dve.tensor_tensor(headsel[:], part_b[:], part_c[:], ALU.is_equal))
            dve.wait_ge(s["k_ps"], 1)
            dve.tensor_scalar(kT[:], bank[3][:, 0:B * S2].rearrange("p (b k) -> p b k", b=B), col_sb[:, 1:2], None,
                              ALU.add).then_inc(s["kT_s"], 1)
            dve.wait_ge(s["kT_s"], 1)
            dve.wait_ge(s["kz_s"], 1)
            for b in range(B):
                dve.tensor_tensor(kblock[:, b, :, 0:S2], kT[:, b:b + 1, :].to_broadcast([P, HG, S2]),
                                  headsel[:].rearrange("p (i a) -> p i a", a=1).to_broadcast([P, HG, S2]),
                                  ALU.mult).then_inc(s["kb_s"], 1)
            dve.wait_ge(s["v_ps"], 1)
            dve.wait_ge(s["kv_in"], 48)
            dve.wait_ge(s["vz_s"], 1)
            for b in range(B):
                for i in range(HG):
                    dve.tensor_tensor(
                        v_pad[:, b, :, i, i, :],
                        bank[6 + b][0:S2, 0:D].rearrange("p (g i d) -> p g i d", g=G, i=HG)[:, :, i, :],
                        bv_sb[:].rearrange("p (g i d) -> p g i d", g=G, i=HG)[:, :, i, :], ALU.add)\
                        .then_inc(s["v_s"], 1)
            dve.wait_ge(s["tanh_s"], 1)
            for t in range(NT):
                dve.scalar_tensor_tensor(out=xb[:, t, :], in0=bo_sb[:], scalar=tanh_g[:, 0:1], in1=x_sb[:, t, :],
                                         op0=ALU.mult, op1=ALU.add).then_inc(s["xb_s"], 1)

            def soft_sum(t):
                u = t % 2
                dve.wait_ge(s["exp_s"], t + 1)
                dve.tensor_reduce(sums[:, u, :], expd[:, u], AX_X, ALU.add).then_inc(s["sum_s"], 1)
                dve.wait_ge(s["sum_s"], t + 1)
                dve.reciprocal(rsum[:, u, :], sums[:, u, :]).then_inc(s["rsum_s"], 1)
                dve.wait_ge(s["rsum_s"], t + 1)
                if t >= 2:
                    dve.wait_ge(s["r_ps"], t - 1)
                dve.tensor_copy(rsum_wide[:, u], rsum[:, u, :].rearrange("p (h a) -> p h a", a=1)
                                .to_broadcast([P, H, DH])).then_inc(s["rwide_s"], 1)

            def normalise(t):
                u = t % 2
                dve.wait_ge(s["r_sb"], t + 1)
                if t >= 2:
                    dve.wait_ge(s["y_ps"], t - 1)
                dve.tensor_tensor(attT[:, u], bank[6][:, 0:P], rsumT[:, u], ALU.mult).then_inc(s["att_s"], 1)

            def residual(t):
                dve.wait_ge(s["y_ps"], t + 1)
                if t == 0:
                    dve.wait_ge(s["xb_s"], NT)
                dve.scalar_tensor_tensor(out=x1[:, t, :], in0=bank[7][:, 0:D], scalar=tanh_g[:, 0:1], in1=xb[:, t, :],
                                         op0=ALU.mult, op1=ALU.add).then_inc(s["x1_s"], 1)

            def stats_2(t):
                dve.wait_ge(s["x1_s"], t + 1)
                dve.bn_stats(stats2[:, t, :], x1[:, t, :]).then_inc(s["st2_s"], 1)

            for t in range(NT + 4):
                if t < NT:
                    u = t % 2
                    dve.wait_ge(s["score_s"], t + 1)
                    for g in range(G):
                        m = dve.tensor_reduce(top[:, u, g * HG:(g + 1) * HG],
                                              bank[g][:, 0:HG * KP].rearrange("p (i k) -> p i k", i=HG)[:, :, 0:S2],
                                              AX_X, ALU.max)
                    m.then_inc(s["max_s"], 1)
                    dve.wait_ge(s["max_s"], t + 1)
                    if t >= 2:
                        dve.wait_ge(s["exp_s"], t - 1)
                    for g in range(G):
                        m = dve.tensor_tensor(shifted[:, u, g * HG:(g + 1) * HG, :],
                                              bank[g][:, 0:HG * KP].rearrange("p (i k) -> p i k", i=HG)[:, :, 0:S2],
                                              top[:, u, g * HG:(g + 1) * HG].rearrange("p (i a) -> p i a", a=1)
                                              .to_broadcast([P, HG, S2]), ALU.subtract)
                    m.then_inc(s["shift_s"], 1)
                if 1 <= t < NT + 1:
                    soft_sum(t - 1)
                if 3 <= t < NT + 3:
                    normalise(t - 3)
                if t >= 4:
                    residual(t - 4)
                if t >= 5:
                    stats_2(t - 5)
            stats_2(NT - 1)

            for t in range(NT):
                dve.wait_ge(s["st2_s"], t + 1)
                dve.bn_aggr(meanvar2[:, t, :], stats2[:, t, :]).then_inc(s["mv2_s"], 1)
            dve.wait_ge(s["mv2_s"], NT)
            dve.tensor_scalar(veps2[:], meanvar2[:, :, 1], EPS, None, ALU.add).then_inc(s["ve2_s"], 1)
            dve.wait_ge(s["rs2_s"], 1)
            step(dve.tensor_tensor(rr[:], rstd2[:], rstd2[:], ALU.mult))
            step(dve.tensor_tensor(rr[:], rr[:], meanvar2[:, :, 1], ALU.mult))
            dve.tensor_scalar(veps3[:], rr[:], EPS, None, ALU.add).then_inc(s["ve3_s"], 1)
            dve.wait_ge(s["ve3_s"], 1)
            dve.wait_ge(s["rs3_s"], 1)
            step(dve.tensor_tensor(rr[:], rstd2[:], rstd3[:], ALU.mult))
            for t in range(NT):
                dve.tensor_scalar(z2[:, t, :], x1[:, t, :], meanvar2[:, t, 0:1], rr[:, t:t + 1],
                                  ALU.subtract, ALU.mult).then_inc(s["z2_s"], 1)
            dve.wait_ge(s["iota_s"], 5)
            dve.tensor_copy(iota_f[:], iota_i[:])
            dve.tensor_copy(tok_f[:], tok_i[:])
            dve.tensor_copy(row_f[:], row_i[:])
            step(dve.tensor_copy(dump_f[:], dump_i[:]))

            dve.wait_ge(s["log_ps"], 1)
            step(dve.tensor_copy(logit[:], bank[2][:, 0:NT * E].rearrange("p (t e) -> p t e", t=NT)))
            for t in range(NT):
                m = dve.max(best[:, t, :], logit[:, t, :])
            step(m)
            for t in range(NT):
                m = dve.max_index(best_i[:, t, :], best[:, t, :], logit[:, t, :])
            dve.tensor_tensor(gap[:], best[:, :, 1], best[:, :, 0], ALU.subtract).then_inc(s["gap_s"], 1)
            step(m)
            step(dve.tensor_copy(choice_f[:], best_i[:, :, 0:TOPK].rearrange("p t k -> p k t")))
            for k in range(TOPK):
                m = dve.tensor_tensor(onehot[:, k], iota_f[:, 0:E].rearrange("p (a e) -> p a e", a=1)
                                      .to_broadcast([P, NT, E]),
                                      choice_f[:, k, :].rearrange("p (t a) -> p t a", a=1).to_broadcast([P, NT, E]),
                                      ALU.is_equal)
            step(m)
            dve.tensor_tensor(member[:], onehot[:, 0], onehot[:, 1], ALU.add).then_inc(s["member_s"], 1)

            for b in range(B):
                dve.wait_ge(s["shg_ps"], b + 1)
                dve.tensor_scalar(sh_gate[:, b * S:(b + 1) * S], bank[b][:], -10.0, 10.0, ALU.max, ALU.min)\
                    .then_inc(s["shc_s"], 1)

            dve.wait_ge(s["egap_s"], 1)
            step(dve.tensor_scalar(egap1[:], egap[:], 1.0, None, ALU.add))
            step(dve.reciprocal(wgt[:, 0, :], egap1[:]))
            step(dve.tensor_tensor(wgt[:, 1, :], wgt[:, 0, :], egap[:], ALU.mult))
            step(dve.tensor_scalar(wgt_g[:], wgt[:], tanh_g[:, 1:2], None, ALU.mult))

            dve.wait_ge(s["cnt_ps"], 1)
            step(dve.tensor_scalar(cnt_i[:], bank[6][:, 0:E], float(P - 1), None, ALU.add))
            step(dve.tensor_scalar(tiles_i[:], cnt_i[:], 7, None, ALU.logical_shift_right))
            step(dve.tensor_copy(tiles_f[:], tiles_i[:]))
            dve.wait_ge(s["const"], 7)
            step(dve.tensor_tensor(tiles_sq[:], upto[:], tiles_f[:].rearrange("p (a e) -> p a e", a=1)
                                   .to_broadcast([P, E, E]), ALU.mult))
            step(dve.tensor_reduce(tiles_incl[:], tiles_sq[:], AX_X, ALU.add))
            step(dve.tensor_tensor(tiles_excl[:], tiles_incl[:], tiles_f[:], ALU.subtract))
            step(dve.tensor_scalar(start[:], tiles_excl[:], float(P), None, ALU.mult))
            dve.wait_ge(s["rank_ps"], 1)
            step(dve.tensor_tensor(slot_te[:], bank[3][:, 0:NT * E].rearrange("p (t e) -> p t e", t=NT),
                                   start[:].rearrange("p (a e) -> p a e", a=1).to_broadcast([P, NT, E]), ALU.add))
            for k in range(TOPK):
                m = dve.tensor_tensor(slot_sel[:, k], onehot[:, k], slot_te[:], ALU.mult)
            step(m)
            step(dve.tensor_reduce(slot_f[:], slot_sel[:].rearrange("p k t e -> p (k t) e"), AX_X, ALU.add))
            step(dve.tensor_copy(slot_i[:], slot_f[:]))
            dve.tensor_scalar(sj_i[:], slot_i[:], 7, None, ALU.logical_shift_right)
            step(dve.tensor_scalar(sr_i[:], slot_i[:], P - 1, None, ALU.bitwise_and))
            dve.tensor_copy(sj_f[:], sj_i[:])
            step(dve.tensor_copy(sr_f[:], sr_i[:]))
            dve.tensor_copy(vals[:, :, 0], tok_f[:])
            dve.tensor_copy(vals[:, :, 2], wgt_g[:].rearrange("p k t -> p (k t)"))
            step(dve.tensor_tensor(vals[:, :, 1], slot_f[:], row_f[:], ALU.subtract))
            step(dve.tensor_scalar(vals[:, :, 1], vals[:, :, 1], float(TOPK * TOK), None, ALU.add))
            step(dve.tensor_tensor(hot_j[:], iota_f[:, 0:JC].rearrange("p (a j) -> p a j", a=1).to_broadcast([P, PAIRS, JC]),
                                   sj_f[:].rearrange("p (n a) -> p n a", a=1).to_broadcast([P, PAIRS, JC]), ALU.is_equal))
            dve.tensor_tensor(hot_r, iota_f[:].rearrange("p (a r) -> p a r", a=1).to_broadcast([P, PAIRS, P]),
                              sr_f[:].rearrange("p (n a) -> p n a", a=1).to_broadcast([P, PAIRS, P]), ALU.is_equal)
            for v in range(3):
                m = dve.tensor_tensor(hot_v[:, :, v, :], hot_j[:], vals[:, :, v:v + 1].to_broadcast([P, PAIRS, JC]),
                                      ALU.mult)
            m.then_inc(s["vals_s"], 1)
            step(dve.tensor_tensor(past[:], tiles_incl[:].rearrange("p (a e) -> p a e", a=1).to_broadcast([P, JC, E]),
                                   iota_f[:, 0:JC].rearrange("p (j a) -> p j a", a=1).to_broadcast([P, JC, E]),
                                   ALU.is_le))
            step(dve.tensor_reduce(exp_f[:], past[:], AX_X, ALU.add))
            step(dve.tensor_scalar(exp_c[:], exp_f[:], float(E - 1), None, ALU.min))
            dve.tensor_copy(exp_i[:], exp_c[:]).then_inc(s["expert_s"], 1)
            dve.wait_ge(s["list_ps"], 1)
            dve.tensor_copy(gidx[:], bank[7][:, 0:JC]).then_inc(s["list_s"], 1)
            dve.tensor_tensor(sidx[:], dump_f[:], bank[7][:, JC:2 * JC], ALU.subtract)\
                .then_inc(s["list_s"], 1)
            dve.tensor_copy(wslot[:], bank[7][:, 2 * JC:3 * JC]).then_inc(s["list_s"], 1)

            for b in range(B):
                c = slice(b * S, (b + 1) * S)
                dve.wait_ge(s["shsilu_s"], b + 1)
                dve.tensor_tensor(sh_hT[:, c], bank[4 + b][:], sh_silu[:, c], ALU.mult).then_inc(s["shh_s"], 1)
            for t in range(NT):
                b = t // TPB
                dve.wait_ge(s["shd_ps"], b + 1)
                dve.scalar_tensor_tensor(out=base[:, t, :], in0=bank[b][:, (t % TPB) * D:(t % TPB + 1) * D],
                                         scalar=tanh_g[:, 1:2], in1=x1[:, t, :], op0=ALU.mult, op1=ALU.add)\
                    .then_inc(s["base_s"], 1)

            def rows_copy(j, u):
                dve.wait_ge(s["xgT_ps"], j + 1)
                if not isinstance(j, int) or j > 1:
                    dve.wait_ge(s["gu_ps"], (j - 1) * 2)
                dve.tensor_scalar(xgT[:, u], bank[0][:, 0:P], col_sb[:, 2:3], col_sb[:, 3:4], ALU.mult, ALU.add)\
                    .then_inc(s["xgT_s"], 1)

            def clip_tile(j, u):
                dve.wait_ge(s["gu_ps"], j * 2 + 1)
                if not isinstance(j, int) or j > 1:
                    dve.wait_ge(s["silu_s"], j - 1)
                dve.tensor_scalar(gate[:, u], bank[2 + u][:], -10.0, 10.0, ALU.max, ALU.min).then_inc(s["clip_s"], 1)

            def hid_tile(j, u):
                dve.wait_ge(s["silu_s"], j + 1)
                dve.wait_ge(s["gu_ps"], j * 2 + 2)
                if not isinstance(j, int) or j > 1:
                    dve.wait_ge(s["hT_ps"], j - 1)
                dve.tensor_tensor(hid[:, u], bank[4 + u][:], silu[:, u], ALU.mult).then_inc(s["hid_s"], 1)

            rows_copy(0, 0)
            rows_copy(1, 1)
            clip_tile(0, 0)
            hid_tile(0, 0)
            rows_copy(2, 0)
            clip_tile(1, 1)
            hid_tile(1, 1)
            with dve.Fori(0, (SLOT_TILES - 3) // 2) as i:
                for v in range(2):
                    rows_copy(i * 2 + (3 + v), (3 + v) % 2)
                    clip_tile(i * 2 + (2 + v), v % 2)
                    hid_tile(i * 2 + (2 + v), v % 2)
            clip_tile(SLOT_TILES - 1, 0)
            hid_tile(SLOT_TILES - 1, 0)

            dve.wait_ge(s["chosen_s"], 16)
            dve.tensor_tensor(sum1[:], base[:], chosen[:, 0], ALU.add).then_inc(s["sum1_s"], 1)
            dve.wait_ge(s["sum1_s"], 1)
            dve.tensor_tensor(result[:], sum1[:], chosen[:, 1], ALU.add).then_inc(s["result_s"], 1)


_INS = ['x', 'ctx_1024', 'fside_BxSxS2_0', 'mask_BxSxS2_ik1', 'g_xattn', 'g_ffn', 'L0_xattn_wq_k', 'L0_xattn_wq_b',
        'L0_xattn_wk_k', 'L0_xattn_wk_b', 'L0_xattn_wv_k', 'L0_xattn_wv_b', 'L0_xattn_wo_k', 'L0_xattn_wo_b',
        'L0_ffn_ln_gamma', 'L0_ffn_ln_beta', 'L0_ffn_router_w', 'L0_ffn_gate_up_w', 'L0_ffn_down_w',
        'L0_ffn_shared_gate_up_w', 'L0_ffn_shared_down_w']


def kernel(**inputs):
    import numpy as _np
    import concourse.bacc as _bacc
    from concourse import mybir as _mybir
    from concourse.bass_utils import run_bass_kernel_spmd as _run

    nc = _bacc.Bacc("TRN2", target_bir_lowering=False, num_devices=1)
    arrays, args = {}, []
    for name in _INS:
        a = _np.ascontiguousarray(inputs[name])
        arrays[f"in_{name}_dram"] = a
        args.append(nc.dram_tensor(f"in_{name}_dram", a.shape, _mybir.dt.from_np(a.dtype), kind="ExternalInput").ap())
    shape = inputs["x"].shape
    args.append(nc.dram_tensor("out_0_dram", shape, _mybir.dt.float32, kind="ExternalOutput").ap())
    gated_block(nc, *args)
    r = _run(nc, [arrays], core_ids=[0])
    return r.results[0]["out_0_dram"]
```

```python
from contextlib import ExitStack

import concourse.bass as bass
from concourse import mybir

ALU = mybir.AluOpType
ACT = mybir.ActivationFunctionType
F32 = mybir.dt.float32
F32R = mybir.dt.float32r
BF16 = mybir.dt.bfloat16
I32 = mybir.dt.int32
U32 = mybir.dt.uint32
AX_X = mybir.AxisListType.X


def gated_block(nc, x, ctx_in, group_prob, mask, g_xattn, g_ffn, wq, bq, wk, bk, wv, bv, wo, bo,
                ln_gamma, ln_beta, router_w, gate_up_w, down_w, sh_gate_up_w, sh_down_w, out):
    P = 128
    B, S, D = x.shape
    S2 = ctx_in.shape[1]
    KP = S2 + S2 % 2
    H, DH = 16, D // 16
    G = 4
    HG = H // G
    TPB = S // P
    NT = B * TPB
    TOK = B * S
    E, F = down_w.shape[0], down_w.shape[1]
    FS = sh_down_w.shape[0]
    FC = F // P
    TOPK = 2
    PAIRS = TOPK * NT
    SLOT_TILES = TOK * TOPK // P + E - 1
    JC = SLOT_TILES + SLOT_TILES % 2
    EPS = 1e-5
    SP = 3 * P // G
    QSCALE = float(DH) ** -0.5
    assert D == P and FS == P and H == G * HG and HG * KP <= 512

    x_tiles = x.rearrange("b (t p) d -> p (b t) d", p=P)
    gp_tiles = group_prob.rearrange("b (t p) k -> p (b t) k", p=P)
    mask_tiles = mask.rearrange("b (t p) k -> p (b t) k", p=P)
    out_tiles = out.rearrange("b (t p) d -> p (b t) d", p=P)
    normed_dram = nc.dram_tensor("normed_rows", (TOK, D), F32, kind="Internal").ap()
    chosen_dram = nc.dram_tensor("chosen_rows", (TOPK * TOK + SLOT_TILES * P, D), F32, kind="Internal").ap()

    with ExitStack() as ctx:
        def sb(name, shape, dt=F32):
            return ctx.enter_context(nc.sbuf_tensor(name, shape, dt))

        attention = ExitStack()

        def at(name, shape, dt=F32):
            return attention.enter_context(nc.sbuf_tensor(name, shape, dt))

        def sem(name):
            return ctx.enter_context(nc.semaphore(name))

        quad = ctx.enter_context(nc.psum_tensor("banks0to3", [P, 4, 512], F32))
        bank = [quad[:, i, :] for i in range(4)] + \
            [ctx.enter_context(nc.psum_tensor(f"bank{i}", [P, 512], F32))[:] for i in range(4, 8)]

        x_sb = sb("x_sb", [P, NT, D])
        wo_sb = sb("wo_sb", [P, D])
        col_sb = sb("col_sb", [P, 2])
        gates_sb = sb("gates_sb", [P, 2])
        router_sb = sb("router_sb", [P, E])
        gu_sb = sb("gu_sb", [P, E * 2 * F])
        down_sb = sb("down_sb", [P, E * FC * D])
        shgu_sb = sb("shgu_sb", [P, 2 * FS])
        shdown_sb = sb("shdown_sb", [P, D])
        ident = sb("ident", [P, P])
        ident_r = sb("ident_r", [P, P], F32R)
        earlier = sb("earlier", [P, P], BF16)
        ones = sb("ones", [P, P], BF16)
        upto = sb("upto", [P, E, E])
        iota_i = sb("iota_i", [P, P], I32)
        iota_f = sb("iota_f", [P, P])
        row_i = sb("row_i", [P, PAIRS], I32)
        row_f = sb("row_f", [P, PAIRS])
        dump_i = sb("dump_i", [P, JC], I32)
        dump_f = sb("dump_f", [P, JC])
        neghalf = sb("neghalf", [P, NT])
        z_sb = sb("z_sb", [P, NT, D])
        zT = sb("zT", [P, TOK])
        tanh_g = sb("tanh_g", [P, 2])
        xb = sb("xb", [P, NT, D])
        x1 = sb("x1", [P, NT, D])

        ctx_sb = at("ctx_sb", [S2, B, D])
        gp_sb = at("gp_sb", [P, NT, S2])
        mask_sb = at("mask_sb", [P, NT, S2], I32)
        wq_sb, wk_sb, wv_sb = (at(n, [P, D]) for n in ("wq_sb", "wk_sb", "wv_sb"))
        wq3 = at("wq3", [P, G, 3, P // G])
        wk3 = at("wk3", [P, G, 3, P // G])
        bq_sb = at("bq_sb", [SP, G])
        bk_sb = at("bk_sb", [SP, G])
        bv_sb = at("bv_sb", [S2, D])
        bo_sb = at("bo_sb", [P, D])
        part_i = at("part_i", [SP, HG], I32)
        part_b = at("part_b", [SP, HG], I32)
        headsel = at("headsel", [SP, HG])
        stats = at("stats", [P, NT, 6])
        meanvar = at("meanvar", [P, NT, 2])
        veps = at("veps", [P, NT])
        rstd = at("rstd", [P, NT])
        q_stack = at("q_stack", [SP, G, TOK], F32R)
        ctxT = at("ctxT", [P, B, S2])
        k_full = at("k_full", [SP, G, B, S2])
        k_hi = at("k_hi", [SP, G, B, S2], F32R)
        k_stack = at("k_stack", [SP, G, B, HG, KP], F32R)
        v_pad = at("v_pad", [S2, B, G, HG, HG, DH])
        neg = at("neg", [P, NT, S2])
        neg_hi = at("neg_hi", [P, NT, KP], F32R)
        neg_lo = at("neg_lo", [P, NT, KP], F32R)
        bo_g = at("bo_g", [P, D])
        top = at("top", [P, 2, H])
        shifted = at("shifted", [P, 2, H, S2])
        expd = at("expd", [P, 2, H, S2])
        prob = at("prob", [P, 2, H, S2])
        probT = at("probT", [P, 2, HG, G, P])
        sums = at("sums", [P, 2, H])
        rsum = at("rsum", [P, 2, H])
        rsum_wide = at("rsum_wide", [P, 2, H, DH])
        rsumT = at("rsumT", [P, 2, P])
        attT = at("attT", [P, 2, P])
        attention.close()

        stats2 = sb("stats2", [P, NT, 6])
        meanvar2 = sb("meanvar2", [P, NT, 2])
        veps2 = sb("veps2", [P, NT])
        rstd2 = sb("rstd2", [P, NT])
        veps3 = sb("veps3", [P, NT])
        rstd3 = sb("rstd3", [P, NT])
        rr = sb("rr", [P, NT])
        z2 = z_sb
        x2T = zT
        logit = sb("logit", [P, NT, E])
        best = sb("best", [P, NT, 8])
        best_i = sb("best_i", [P, NT, 8], U32)
        choice_f = sb("choice_f", [P, TOPK, NT])
        onehot = sb("onehot", [P, TOPK, NT, E])
        member = sb("member", [P, NT, E], BF16)
        gap = sb("gap", [P, NT])
        egap = sb("egap", [P, NT])
        egap1 = sb("egap1", [P, NT])
        wgt = sb("wgt", [P, TOPK, NT])
        wgt_g = sb("wgt_g", [P, TOPK, NT])
        cnt_i = sb("cnt_i", [P, E], I32)
        tiles_i = sb("tiles_i", [P, E], I32)
        tiles_f = sb("tiles_f", [P, E])
        tiles_sq = sb("tiles_sq", [P, E, E])
        tiles_incl = sb("tiles_incl", [P, E])
        tiles_excl = sb("tiles_excl", [P, E])
        start = sb("start", [P, E])
        slot_te = sb("slot_te", [P, NT, E])
        slot_sel = sb("slot_sel", [P, TOPK, NT, E])
        slot_f = sb("slot_f", [P, PAIRS])
        slot_i = sb("slot_i", [P, PAIRS], I32)
        sj_i = sb("sj_i", [P, PAIRS], I32)
        sr_i = sb("sr_i", [P, PAIRS], I32)
        sj_f = sb("sj_f", [P, PAIRS])
        sr_f = sb("sr_f", [P, PAIRS])
        hot_rt = sb("hot_r", [P, PAIRS, P], F32R)
        hot_r = hot_rt[:]
        hot_j = sb("hot_j", [P, PAIRS, JC])
        w_hi = sb("w_hi", [P, PAIRS], F32R)
        vals = sb("vals", [P, PAIRS, 4])
        hot_v = sb("hot_v", [P, PAIRS, 4, JC], F32R)
        row_l = sb("row_l", [P, JC])
        row_li = sb("row_li", [P, JC], I32)
        used = sb("used", [P, JC])
        gidx = sb("gidx", [P, JC], I32)
        sidx = sb("sidx", [P, JC], I32)
        wslot = sb("wslot", [P, JC])
        past = sb("past", [P, JC, E])
        exp_f = sb("exp_f", [P, JC])
        exp_c = sb("exp_c", [P, JC])
        exp_i = sb("exp_i", [P, JC], I32)

        sh_gate = sb("sh_gate", [P, TOK])
        sh_silu = sb("sh_silu", [P, TOK])
        sh_hT = sb("sh_hT", [P, TOK])
        base = sb("base", [P, NT, D])

        xg = sb("xg", [P, 2, D])
        xgT = sb("xgT", [P, 2, P])
        gate = sb("gate", [P, 2, F])
        silu = sb("silu", [P, 2, F])
        hid = sb("hid", [P, 2, F])
        hidT = sb("hidT", [P, 2, F])
        y_all = sb("y_all", [P, SLOT_TILES, D])
        chosen = sb("chosen", [P, TOPK, NT, D])
        sum1 = xb
        result = x_sb

        names = """x_in0 x_in1 ctx_in kv_in q_in col_in bias_in gp_in mask_in small_in sh_in gate_in
            w_in const iota_s headsel_s ident_s identr_s
            stats_s mv_s veps_s rstd_s z_s zT_ps zT_sb q_ps qhi_s qlo_s
            ctxT_ps ctxT_sb wq3_s wk3_s k_ps kf_s khi_s klo_s ks_s kz_s v_ps vz_s v_s neg_s negz_s neghi_s neglo_s tanh_s bog_s xb_s hotr_s
            score_s max_s shift_s exp_s prob_s pt_ps pt_sb o_ps r_ps r_sb sum_s rsum_s rwide_s
            att_s y_ps x1_s st2_s mv2_s ve2_s rs2_s ve3_s rs3_s rr_s z2_s z2_out x2_ps x2_s
            log_ps dstep gap_s egap_s member_s rank_ps cnt_ps vals_s list_ps list_s expert_s
            shg_ps shc_s shsilu_s shh_s shd_ps base_s
            xg_s0 xg_s1 xgT_ps xgT_s gu_ps clip_s silu_s hid_s hT_ps hT_s yy_ps yy_s
            scat_s chosen_s sum1_s result_s out_s""".split()
        s = {n: sem(n) for n in names}

        block = ctx.enter_context(nc.Block())

        @block.sync
        def _(sp):
            sp.dma_start(x_sb[:, 0:TPB, :], x_tiles[:, 0:TPB, :]).then_inc(s["x_in0"], 16)
            sp.dma_start(wq_sb[:], wq).then_inc(s["q_in"], 16)
            sp.dma_start(x_sb[:, TPB:NT, :], x_tiles[:, TPB:NT, :]).then_inc(s["x_in1"], 16)
            sp.dma_start(gp_sb[:], gp_tiles).then_inc(s["gp_in"], 16)
            sp.dma_start(wo_sb[:], wo).then_inc(s["small_in"], 16)
            sp.dma_start(router_sb[:], router_w).then_inc(s["small_in"], 16)
            sp.dma_start(shgu_sb[:], sh_gate_up_w).then_inc(s["sh_in"], 16)
            sp.dma_start(shdown_sb[:], sh_down_w).then_inc(s["sh_in"], 16)
            for e in range(E):
                sp.dma_start(gu_sb[:, e * 2 * F:(e + 1) * 2 * F], gate_up_w[e]).then_inc(s["w_in"], 16)
                sp.dma_start(down_sb[:, e * FC * D:(e + 1) * FC * D].rearrange("p (c d) -> p c d", c=FC),
                             down_w[e].rearrange("(c p) d -> p c d", p=P)).then_inc(s["w_in"], 16)
            sp.wait_ge(s["z2_s"], NT)
            sp.dma_start(normed_dram.rearrange("(t p) d -> p t d", p=P), z2[:]).then_inc(s["z2_out"], 16)
            sp.wait_ge(s["scat_s"], 16 * SLOT_TILES)
            sp.dma_start(chosen[:], chosen_dram[0:TOPK * TOK, :].rearrange("(k t p) d -> p k t d", k=TOPK, p=P))\
                .then_inc(s["chosen_s"], 16)
            sp.wait_ge(s["result_s"], 1)
            sp.dma_start(out_tiles, result[:]).then_inc(s["out_s"], 16)
            sp.wait_ge(s["out_s"], 16)

        @block.gpsimd
        def _(pool):
            pool.memset(neghalf[:], -0.5).then_inc(s["const"], 1)
            pool.memset(ident[:], 0.0).then_inc(s["const"], 1)
            pool.wait_ge(s["const"], 2)
            pool.affine_select(out=ident[:], in_=ident[:], compare_op=ALU.not_equal, fill=1.0, base=0,
                               pattern=[[-1, P]], channel_multiplier=1).then_inc(s["ident_s"], 1)
            pool.iota(part_i[:], [[0, HG]], base=0, channel_multiplier=1).then_inc(s["iota_s"], 1)
            pool.iota(iota_i[:], [[1, P]], base=0, channel_multiplier=0).then_inc(s["iota_s"], 1)
            pool.wait_ge(s["veps_s"], 1)
            pool.tensor_tensor(rstd[:], veps[:], neghalf[:], ALU.pow).then_inc(s["rstd_s"], 1)
            pool.memset(v_pad[:], 0.0).then_inc(s["vz_s"], 1)
            pool.memset(k_stack[:, :, :, :, S2:KP].bitcast(F32), 0.0).then_inc(s["kz_s"], 1)
            pool.iota(row_i[:], [[TOK, TOPK], [P, NT]], base=0, channel_multiplier=1).then_inc(s["iota_s"], 1)
            pool.iota(dump_i[:], [[P, JC]], base=TOPK * TOK, channel_multiplier=1).then_inc(s["iota_s"], 1)
            pool.memset(ones[:], 1.0).then_inc(s["const"], 1)
            pool.memset(earlier[:], 1.0).then_inc(s["const"], 1)
            pool.memset(upto[:], 1.0).then_inc(s["const"], 1)
            pool.wait_ge(s["const"], 5)
            pool.affine_select(out=earlier[:], in_=earlier[:], compare_op=ALU.is_gt, fill=0.0, base=0,
                               pattern=[[1, P]], channel_multiplier=-1).then_inc(s["const"], 1)
            pool.affine_select(out=upto[:], in_=upto[:], compare_op=ALU.is_ge, fill=0.0, base=0,
                               pattern=[[1, E], [-1, E]], channel_multiplier=0).then_inc(s["const"], 1)
            pool.wait_ge(s["bog_s"], 1)
            pool.wait_ge(s["x_in0"], 16)
            pool.wait_ge(s["x_in1"], 16)
            pool.tensor_tensor(xb[:], x_sb[:], bo_g[:].rearrange("p (a d) -> p a d", a=1).to_broadcast([P, NT, D]),
                               ALU.add).then_inc(s["xb_s"], 1)
            pool.wait_ge(s["gp_in"], 16)
            for t in range(NT):
                u = t % 2
                pool.wait_ge(s["exp_s"], t + 1)
                if t >= 2:
                    pool.wait_ge(s["pt_ps"], HG * (t - 1))
                pool.tensor_tensor(prob[:, u], expd[:, u], gp_sb[:, t:t + 1, :].to_broadcast([P, H, S2]),
                                   ALU.mult).then_inc(s["prob_s"], 1)
            pool.wait_ge(s["ve2_s"], 1)
            pool.tensor_tensor(rstd2[:], veps2[:], neghalf[:], ALU.pow).then_inc(s["rs2_s"], 1)
            pool.wait_ge(s["ve3_s"], 1)
            pool.tensor_tensor(rstd3[:], veps3[:], neghalf[:], ALU.pow).then_inc(s["rs3_s"], 1)

            pool.wait_ge(s["z2_out"], 16)
            pool.wait_ge(s["list_s"], 3)

            def gather(j):
                if j >= 2:
                    pool.wait_ge(s["xgT_ps"], j - 1)
                pool.indirect_dma_start(xg[:, j % 2, :], None, normed_dram,
                                        bass.IndirectOffsetOnAxis(ap=gidx[:, j:j + 1], axis=0))\
                    .then_inc(s[f"xg_s{j % 2}"], 16)

            def scatter(j):
                pool.wait_ge(s["yy_s"], j + 1)
                pool.indirect_dma_start(chosen_dram, bass.IndirectOffsetOnAxis(ap=sidx[:, j:j + 1], axis=0),
                                        y_all[:, j, :], None).then_inc(s["scat_s"], 16)

            for j in range(SLOT_TILES):
                gather(j)
                if j >= 5:
                    scatter(j - 5)
            for j in range(SLOT_TILES - 5, SLOT_TILES):
                scatter(j)

        @block.scalar
        def _(act):
            act.dma_start(ctx_sb[:], ctx_in.rearrange("b k d -> k b d")).then_inc(s["ctx_in"], 16)
            act.dma_start(wk_sb[:], wk).then_inc(s["kv_in"], 16)
            act.dma_start(wv_sb[:], wv).then_inc(s["kv_in"], 16)
            act.dma_start(bv_sb[:], bv.rearrange("(a d) -> a d", a=1).to_broadcast([S2, D])).then_inc(s["kv_in"], 16)
            for dst, v in ((bk_sb, bk), (bq_sb, bq)):
                for a in range(3):
                    with nc.allow_non_contiguous_dma(reason="a bias on the partitions of its rows"):
                        act.dma_start(dst[32 * a:32 * a + 32, :], v.rearrange("(g r) -> r g", g=G))\
                            .then_inc(s["bias_in"], 16)
            act.dma_start(mask_sb[:], mask_tiles).then_inc(s["mask_in"], 16)
            act.dma_start(gates_sb[:, 0:1], g_xattn.rearrange("(a d) -> a d", a=1).to_broadcast([P, 1])).then_inc(s["gate_in"], 16)
            act.dma_start(gates_sb[:, 1:2], g_ffn.rearrange("(a d) -> a d", a=1).to_broadcast([P, 1])).then_inc(s["gate_in"], 16)
            for n, v in enumerate((ln_gamma, ln_beta)):
                act.dma_start(col_sb[:, n:n + 1], v.rearrange("(d a) -> d a", a=1)).then_inc(s["col_in"], 16)
            act.dma_start(bo_sb[:], bo.rearrange("(a d) -> a d", a=1).to_broadcast([P, D])).then_inc(s["gate_in"], 16)

            def evac(dst, src):
                return act.activation(dst, src, ACT.Copy)

            def thrice(dst, src):
                return act.activation(dst[:], src[:].rearrange("p (g a r) -> p g a r", g=G, a=1)
                                      .to_broadcast([P, G, 3, P // G]), ACT.Copy)

            act.wait_ge(s["kv_in"], 48)
            thrice(wk3, wk_sb).then_inc(s["wk3_s"], 1)
            act.wait_ge(s["ctxT_ps"], 1)
            evac(ctxT[:], bank[2][:, 0:B * S2].rearrange("p (b k) -> p b k", b=B)).then_inc(s["ctxT_sb"], 1)
            act.wait_ge(s["q_in"], 16)
            thrice(wq3, wq_sb).then_inc(s["wq3_s"], 1)
            for b in range(B):
                act.wait_ge(s["zT_ps"], b + 1)
                evac(zT[:, b * S:(b + 1) * S], bank[4 + b]).then_inc(s["zT_sb"], 1)
                if b == 0:
                    act.wait_ge(s["bias_in"], 96)
                for g in range(G):
                    act.wait_ge(s["q_ps"], b * G + g + 1)
                    act.activation(q_stack[:, g, b * S:(b + 1) * S], bank[g][0:SP, :], ACT.Identity,
                                   bias=bq_sb[:, g:g + 1]).then_inc(s["qhi_s"], 1)
            act.wait_ge(s["gate_in"], 48)
            act.activation(tanh_g[:], gates_sb[:], ACT.Tanh).then_inc(s["tanh_s"], 1)

            def exp_tile(t):
                u = t % 2
                act.wait_ge(s["shift_s"], t + 1)
                if t >= 2:
                    act.wait_ge(s["prob_s"], t - 1)
                    act.wait_ge(s["sum_s"], t - 1)
                act.activation(expd[:, u], shifted[:, u], ACT.Exp).then_inc(s["exp_s"], 1)

            def back_tile(t):
                u = t % 2
                for i in range(HG):
                    act.wait_ge(s["pt_ps"], HG * t + i + 1)
                    if i == 0 and t >= 2:
                        act.wait_ge(s["o_ps"], t - 1)
                    evac(probT[0:S2, u, i], bank[4 + i % 2][0:S2, :].rearrange("p (g q) -> p g q", g=G))\
                        .then_inc(s["pt_sb"], 1)
                act.wait_ge(s["r_ps"], t + 1)
                if t >= 2:
                    act.wait_ge(s["att_s"], t - 1)
                evac(rsumT[:, u], bank[6 + u][:, P:2 * P]).then_inc(s["r_sb"], 1)

            for t in range(NT + 2):
                if t >= 2:
                    back_tile(t - 2)
                if t < NT:
                    exp_tile(t)

            for b in range(B):
                act.wait_ge(s["x2_ps"], b + 1)
                act.activation(x2T[:, b * S:(b + 1) * S], bank[b], ACT.Identity, bias=col_sb[:, 1:2],
                               scale=col_sb[:, 0:1]).then_inc(s["x2_s"], 1)
            act.wait_ge(s["gap_s"], 1)
            act.activation(egap[:], gap[:], ACT.Exp).then_inc(s["egap_s"], 1)
            for b in range(B):
                act.wait_ge(s["shc_s"], b + 1)
                act.activation(sh_silu[:, b * S:(b + 1) * S], sh_gate[:, b * S:(b + 1) * S], ACT.Silu)\
                    .then_inc(s["shsilu_s"], 1)

            def silu_tile(j, u):
                act.wait_ge(s["clip_s"], j + 1)
                act.activation(silu[:, u], gate[:, u], ACT.Silu).then_inc(s["silu_s"], 1)

            def hidT_tile(j, u):
                act.wait_ge(s["hT_ps"], j + 1)
                evac(hidT[:, u], bank[6]).then_inc(s["hT_s"], 1)

            def y_tile(j, u):
                act.wait_ge(s["yy_ps"], j + 1)
                act.activation(y_all[:, bass.ds(j, 1), :].rearrange("p a d -> p (a d)"), bank[7][:, 0:D],
                               ACT.Copy, scale=wslot[:, bass.ds(j, 1)]).then_inc(s["yy_s"], 1)

            act.wait_ge(s["list_s"], 3)
            silu_tile(0, 0)
            silu_tile(1, 1)
            hidT_tile(0, 0)
            silu_tile(2, 0)
            hidT_tile(1, 1)
            y_tile(0, 0)
            with act.Fori(0, (SLOT_TILES - 3) // 2) as i:
                for v in range(2):
                    j = i * 2 + (3 + v)
                    silu_tile(j, (3 + v) % 2)
                    hidT_tile(i * 2 + (2 + v), v % 2)
                    y_tile(i * 2 + (1 + v), (1 + v) % 2)
            hidT_tile(SLOT_TILES - 1, 0)
            y_tile(SLOT_TILES - 2, 1)
            y_tile(SLOT_TILES - 1, 0)

        @block.tensor
        def _(pe):
            pe.wait_ge(s["ident_s"], 1)
            pe.wait_ge(s["ctx_in"], 16)
            for b in range(B):
                m = pe.transpose(bank[2][:, b * S2:(b + 1) * S2], ctx_sb[:, b, :], ident[0:S2, 0:S2])
            m.then_inc(s["ctxT_ps"], 1)
            pe.wait_ge(s["ctxT_sb"], 1)
            pe.wait_ge(s["kv_in"], 48)
            pe.wait_ge(s["wk3_s"], 1)
            for g in range(G):
                m = pe.matmul(bank[4 + g // 2][0:SP, (g % 2) * B * S2:(g % 2 + 1) * B * S2],
                              wk3[:, g].rearrange("p a r -> p (a r)"),
                              ctxT[:].rearrange("p b k -> p (b k)"), start=True, stop=True)
            m.then_inc(s["k_ps"], 1)
            for b in range(B):
                m = pe.matmul(bank[6 + b][0:S2, 0:D], ctxT[:, b, :], wv_sb[:], start=True, stop=True)
            m.then_inc(s["v_ps"], 1)
            pe.wait_ge(s["kf_s"], 1)
            for b in range(B):
                pe.wait_ge(s["z_s"], TPB * (b + 1))
                for t in range(TPB):
                    m = pe.transpose(bank[4 + b][:, t * P:(t + 1) * P], z_sb[:, b * TPB + t, :], ident[:])
                m.then_inc(s["zT_ps"], 1)
            pe.wait_ge(s["wq3_s"], 1)
            for b in range(B):
                pe.wait_ge(s["zT_sb"], b + 1)
                for g in range(G):
                    if b > 0:
                        pe.wait_ge(s["qlo_s"], (b - 1) * G + g + 1)
                        pe.wait_ge(s["qhi_s"], (b - 1) * G + g + 1)
                    pe.matmul(bank[g][0:SP, :],
                              wq3[:, g].rearrange("p a r -> p (a r)"),
                              zT[:, b * S:(b + 1) * S], start=True, stop=True).then_inc(s["q_ps"], 1)

            def scores(t):
                b = t // TPB
                if t == 0:
                    pe.wait_ge(s["identr_s"], 1)
                    pe.wait_ge(s["neglo_s"], 1)
                    pe.wait_ge(s["neghi_s"], 1)
                    pe.wait_ge(s["negz_s"], 2)
                    pe.wait_ge(s["ks_s"], G)
                    pe.wait_ge(s["kz_s"], 1)
                    pe.wait_ge(s["qlo_s"], B * G)
                    pe.wait_ge(s["qhi_s"], B * G)
                else:
                    pe.wait_ge(s["shift_s"], t)
                for g in range(G):
                    dst = bank[g][:, 0:HG * KP]
                    for n, part in enumerate((neg_hi, neg_lo)):
                        pe.matmul(dst, ident_r[:], part[:, t:t + 1, :].to_broadcast([P, HG, KP]),
                                  start=(n == 0), stop=False)
                    m = pe.matmul(dst, q_stack[:, g, t * P:(t + 1) * P],
                                  k_stack[:, g, b].rearrange("p i k -> p (i k)"), start=False, stop=True)
                m.then_inc(s["score_s"], 1)

            def attend(t):
                b, u = t // TPB, t % 2
                pe.wait_ge(s["prob_s"], t + 1)
                if t == 0:
                    pe.wait_ge(s["zT_sb"], B)
                    pe.wait_ge(s["v_s"], B * HG)

                def turn(i):
                    k = HG * t + i
                    if k >= 2:
                        pe.wait_ge(s["pt_sb"], k - 1)
                    for g in range(G):
                        m = pe.transpose(bank[4 + i % 2][0:S2, g * P:(g + 1) * P], prob[:, u, G * g + i, :], ident[:])
                    m.then_inc(s["pt_ps"], 1)

                def weigh(i):
                    pe.wait_ge(s["pt_sb"], HG * t + i + 1)
                    if i == 0 and t >= 2:
                        pe.wait_ge(s["x1_s"], t - 1)
                    for g in range(G):
                        m = pe.matmul(bank[6 + u][32 * g:32 * g + 32, 0:P],
                                      v_pad[:, b, g, i].rearrange("p a d -> p (a d)"), probT[0:S2, u, i, g, :],
                                      start=(i == 0), stop=(i == HG - 1))
                    return m

                turn(0)
                turn(1)
                for i in range(HG):
                    m = weigh(i)
                    if i + 2 < HG:
                        turn(i + 2)
                m.then_inc(s["o_ps"], 1)
                pe.wait_ge(s["rwide_s"], t + 1)
                pe.transpose(bank[6 + u][:, P:2 * P], rsum_wide[:, u].rearrange("p h d -> p (h d)"), ident[:])\
                    .then_inc(s["r_ps"], 1)

            def project(t):
                pe.wait_ge(s["att_s"], t + 1)
                if t == 0:
                    pe.wait_ge(s["small_in"], 32)
                pe.matmul(bank[6 + t % 2][:, 2 * P:2 * P + D], attT[:, t % 2], wo_sb[:], start=True, stop=True).then_inc(s["y_ps"], 1)

            for t in range(NT + 3):
                if t < NT:
                    scores(t)
                if 2 <= t < NT + 2:
                    attend(t - 2)
                if t >= 3:
                    project(t - 3)

            for b in range(B):
                pe.wait_ge(s["z2_s"], TPB * (b + 1))
                for t in range(TPB):
                    m = pe.transpose(bank[b][:, t * P:(t + 1) * P], z2[:, b * TPB + t, :], ident[:])
                m.then_inc(s["x2_ps"], 1)
            for t in range(NT):
                if t % TPB == 0:
                    pe.wait_ge(s["x2_s"], t // TPB + 1)
                m = pe.matmul(bank[2][:, t * E:(t + 1) * E], x2T[:, t * P:(t + 1) * P], router_sb[:],
                              start=True, stop=True)
            m.then_inc(s["log_ps"], 1)
            pe.wait_ge(s["sh_in"], 32)
            pe.wait_ge(s["x2_s"], B)
            for b in range(B):
                pe.matmul(bank[b], shgu_sb[:, 0:FS], x2T[:, b * S:(b + 1) * S], start=True, stop=True)
                pe.matmul(bank[4 + b], shgu_sb[:, FS:2 * FS], x2T[:, b * S:(b + 1) * S], start=True, stop=True)\
                    .then_inc(s["shg_ps"], 1)
            pe.wait_ge(s["member_s"], 1)
            rank = bank[3][:, 0:NT * E]
            for t in range(NT - 1):
                n = NT - 1 - t
                pe.matmul(bank[3][:, (t + 1) * E:NT * E], ones[:], member[:, t:t + 1, :].to_broadcast([P, n, E]),
                          start=(t == 0), stop=False, skip_group_check=True)
            m = pe.matmul(rank, earlier[:], member[:].rearrange("p t e -> p (t e)"), start=False, stop=True,
                          skip_group_check=True)
            m.then_inc(s["rank_ps"], 1)
            for t in range(NT):
                m = pe.matmul(bank[6][:, 0:E], ones[:], member[:, t, :], start=(t == 0), stop=(t == NT - 1))
            m.then_inc(s["cnt_ps"], 1)
            pe.wait_ge(s["hotr_s"], 1)
            pe.wait_ge(s["vals_s"], 1)
            for n in range(PAIRS):
                m = pe.matmul(bank[7][:, 0:4 * JC], hot_r[:, n, :], hot_v[:, n].rearrange("p v j -> p (v j)"),
                              start=(n == 0), stop=(n == PAIRS - 1))
            m.then_inc(s["list_ps"], 1)

            for b in range(B):
                pe.wait_ge(s["shh_s"], b + 1)
                for t in range(TPB):
                    m = pe.matmul(bank[b][:, t * D:(t + 1) * D], sh_hT[:, (b * TPB + t) * P:(b * TPB + t + 1) * P],
                                  shdown_sb[:], start=True, stop=True)
                m.then_inc(s["shd_ps"], 1)

            def rows_tile(j, u, nth):
                pe.wait_ge(s[f"xg_s{u}"], nth * 16)
                if not isinstance(j, int) or j > 0:
                    pe.wait_ge(s["xgT_s"], j)
                pe.transpose(bank[0][:, 0:P], xg[:, u], ident[:]).then_inc(s["xgT_ps"], 1)

            def gate_up_tile(j, u):
                e = pe.value_load(exp_i[0:1, bass.ds(j, 1)], min_val=0, max_val=E - 1)
                pe.wait_ge(s["xgT_s"], j + 1)
                if not isinstance(j, int) or j > 1:
                    pe.wait_ge(s["hid_s"], j - 1)
                pe.matmul(bank[2 + u], xgT[:, u], gu_sb[:, bass.ds(e * (2 * F), F)], start=True, stop=True)\
                    .then_inc(s["gu_ps"], 1)
                pe.matmul(bank[4 + u], xgT[:, u], gu_sb[:, bass.ds(e * (2 * F) + F, F)], start=True, stop=True)\
                    .then_inc(s["gu_ps"], 1)

            def hidden_tile(j, u):
                pe.wait_ge(s["hid_s"], j + 1)
                if not isinstance(j, int) or j > 0:
                    pe.wait_ge(s["hT_s"], j)
                for c in range(FC):
                    m = pe.transpose(bank[6][:, c * P:(c + 1) * P], hid[:, u, c * P:(c + 1) * P], ident[:])
                m.then_inc(s["hT_ps"], 1)

            def down_tile(j, u):
                e = pe.value_load(exp_i[0:1, bass.ds(j, 1)], min_val=0, max_val=E - 1)
                pe.wait_ge(s["hT_s"], j + 1)
                if not isinstance(j, int) or j > 0:
                    pe.wait_ge(s["yy_s"], j)
                for c in range(FC):
                    m = pe.matmul(bank[7][:, 0:D], hidT[:, u, c * P:(c + 1) * P],
                                  down_sb[:, bass.ds(e * (FC * D) + c * D, D)], start=(c == 0), stop=(c == FC - 1))
                m.then_inc(s["yy_ps"], 1)

            pe.wait_ge(s["w_in"], 16 * 2 * E)
            pe.wait_ge(s["expert_s"], 1)
            pe.wait_ge(s["base_s"], NT)
            pe.wait_ge(s["list_s"], 3)
            rows_tile(0, 0, 1)
            rows_tile(1, 1, 1)
            gate_up_tile(0, 0)
            rows_tile(2, 0, 2)
            gate_up_tile(1, 1)
            hidden_tile(0, 0)
            rows_tile(3, 1, 2)
            gate_up_tile(2, 0)
            hidden_tile(1, 1)
            down_tile(0, 0)
            with pe.Fori(0, (SLOT_TILES - 5) // 2) as i:
                for v in range(2):
                    rows_tile(i * 2 + (4 + v), v % 2, i + 3)
                    gate_up_tile(i * 2 + (3 + v), (3 + v) % 2)
                    hidden_tile(i * 2 + (2 + v), v % 2)
                    down_tile(i * 2 + (1 + v), (1 + v) % 2)
            for j in range(SLOT_TILES - 2, SLOT_TILES + 2):
                if j + 1 < SLOT_TILES:
                    rows_tile(j + 1, (j + 1) % 2, (j + 1) // 2 + 1)
                if j < SLOT_TILES:
                    gate_up_tile(j, j % 2)
                if j - 1 < SLOT_TILES:
                    hidden_tile(j - 1, (j - 1) % 2)
                down_tile(j - 2, j % 2)

        @block.vector
        def _(dve):
            steps = [0]

            def step(ins):
                steps[0] += 1
                ins.then_inc(s["dstep"], 1)
                dve.wait_ge(s["dstep"], steps[0])

            def layer_stats(b, src, st, mv, name_st):
                for t in range(b * TPB, (b + 1) * TPB):
                    dve.bn_stats(st[:, t, :], src[:, t, :]).then_inc(s[name_st], 1)
                for t in range(b * TPB, (b + 1) * TPB):
                    dve.wait_ge(s[name_st], t + 1)
                    dve.bn_aggr(mv[:, t, :], st[:, t, :]).then_inc(s["mv_s"], 1)

            for b in range(B):
                dve.wait_ge(s[f"x_in{b}"], 16)
                layer_stats(b, x_sb, stats, meanvar, "stats_s")
            dve.wait_ge(s["mv_s"], NT)
            dve.tensor_scalar(veps[:], meanvar[:, :, 1], EPS, None, ALU.add).then_inc(s["veps_s"], 1)
            dve.memset(neg_hi[:, :, S2:KP].bitcast(F32), 0.0).then_inc(s["negz_s"], 1)
            dve.memset(neg_lo[:, :, S2:KP].bitcast(F32), 0.0).then_inc(s["negz_s"], 1)
            dve.wait_ge(s["mask_in"], 16)
            step(dve.tensor_scalar(neg[:], mask_sb[:], -1.0, 1e9, ALU.add, ALU.mult))
            dve.tensor_copy(neg_hi[:, :, 0:S2], neg[:]).then_inc(s["neghi_s"], 1)
            dve.wait_ge(s["neghi_s"], 1)
            dve.tensor_tensor(neg_lo[:, :, 0:S2], neg[:], neg_hi[:, :, 0:S2].bitcast(F32), ALU.subtract)\
                .then_inc(s["neglo_s"], 1)
            dve.wait_ge(s["ident_s"], 1)
            dve.tensor_copy(ident_r[:], ident[:]).then_inc(s["identr_s"], 1)
            dve.wait_ge(s["rstd_s"], 1)
            for t in range(NT):
                dve.tensor_scalar(z_sb[:, t, :], x_sb[:, t, :], meanvar[:, t, 0:1], rstd[:, t:t + 1],
                                  ALU.subtract, ALU.mult).then_inc(s["z_s"], 1)
            dve.wait_ge(s["iota_s"], 2)
            step(dve.tensor_scalar(part_b[:], part_i[:], 3, HG - 1, ALU.logical_shift_right, ALU.bitwise_and))
            step(dve.tensor_tensor(headsel[:], part_b[:], iota_i[0:SP, 0:HG], ALU.is_equal))
            dve.wait_ge(s["k_ps"], 1)
            dve.wait_ge(s["bias_in"], 96)
            for g in range(G):
                m = dve.tensor_scalar(k_full[:, g], bank[4 + g // 2][0:SP, (g % 2) * B * S2:(g % 2 + 1) * B * S2]
                                      .rearrange("p (b k) -> p b k", b=B), bk_sb[:, g:g + 1], QSCALE,
                                      ALU.add, ALU.mult)
            m.then_inc(s["kf_s"], 1)
            dve.wait_ge(s["kf_s"], 1)
            low = slice(2 * P // G, SP)
            dve.tensor_copy(k_hi[low], k_full[low]).then_inc(s["khi_s"], 1)
            dve.wait_ge(s["khi_s"], 1)
            dve.tensor_tensor(k_full[low], k_full[low], k_hi[low].bitcast(F32), ALU.subtract).then_inc(s["klo_s"], 1)
            dve.wait_ge(s["klo_s"], 1)
            for g in range(G):
                for b in range(B):
                    m = dve.tensor_tensor(k_stack[:, g, b, :, 0:S2],
                                          k_full[:, g, b:b + 1, :].to_broadcast([SP, HG, S2]),
                                          headsel[:].rearrange("p (i a) -> p i a", a=1).to_broadcast([SP, HG, S2]),
                                          ALU.mult)
                m.then_inc(s["ks_s"], 1)
            dve.wait_ge(s["v_ps"], 1)
            dve.wait_ge(s["kv_in"], 48)
            dve.wait_ge(s["vz_s"], 1)
            for b in range(B):
                for i in range(HG):
                    dve.tensor_tensor(
                        v_pad[:, b, :, i, i, :],
                        bank[6 + b][0:S2, 0:D].rearrange("p (g i d) -> p g i d", g=G, i=HG)[:, :, i, :],
                        bv_sb[:].rearrange("p (g i d) -> p g i d", g=G, i=HG)[:, :, i, :], ALU.add)\
                        .then_inc(s["v_s"], 1)
            mid = slice(P // G, 2 * P // G)
            for b in range(B):
                for g in range(G):
                    dve.wait_ge(s["qhi_s"], b * G + g + 1)
                    q_mid = q_stack[mid, g, b * S:(b + 1) * S]
                    dve.scalar_tensor_tensor(out=q_mid, in0=bank[g][mid, :], scalar=bq_sb[mid, g:g + 1],
                                             in1=q_mid.bitcast(F32), op0=ALU.add, op1=ALU.subtract)\
                        .then_inc(s["qlo_s"], 1)
            dve.wait_ge(s["tanh_s"], 1)
            dve.wait_ge(s["gate_in"], 48)
            dve.tensor_scalar(bo_g[:], bo_sb[:], tanh_g[:, 0:1], None, ALU.mult).then_inc(s["bog_s"], 1)

            def soft_sum(t):
                u = t % 2
                dve.wait_ge(s["exp_s"], t + 1)
                dve.tensor_reduce(sums[:, u, :], expd[:, u], AX_X, ALU.add).then_inc(s["sum_s"], 1)
                dve.wait_ge(s["sum_s"], t + 1)
                dve.reciprocal(rsum[:, u, :], sums[:, u, :]).then_inc(s["rsum_s"], 1)
                dve.wait_ge(s["rsum_s"], t + 1)
                if t >= 2:
                    dve.wait_ge(s["r_ps"], t - 1)
                dve.tensor_copy(rsum_wide[:, u], rsum[:, u, :].rearrange("p (h a) -> p h a", a=1)
                                .to_broadcast([P, H, DH])).then_inc(s["rwide_s"], 1)

            def normalise(t):
                u = t % 2
                dve.wait_ge(s["r_sb"], t + 1)
                if t >= 2:
                    dve.wait_ge(s["y_ps"], t - 1)
                dve.tensor_tensor(attT[:, u], bank[6 + u][:, 0:P], rsumT[:, u], ALU.mult).then_inc(s["att_s"], 1)

            def residual(t):
                dve.wait_ge(s["y_ps"], t + 1)
                if t == 0:
                    dve.wait_ge(s["xb_s"], 1)
                dve.scalar_tensor_tensor(out=x1[:, t, :], in0=bank[6 + t % 2][:, 2 * P:2 * P + D], scalar=tanh_g[:, 0:1], in1=xb[:, t, :],
                                         op0=ALU.mult, op1=ALU.add).then_inc(s["x1_s"], 1)

            def stats_2(t):
                dve.wait_ge(s["x1_s"], t + 1)
                dve.bn_stats(stats2[:, t, :], x1[:, t, :]).then_inc(s["st2_s"], 1)

            score_view = quad[:, :, 0:HG * KP].rearrange("p g (i k) -> p g i k", i=HG)[:, :, :, 0:S2]

            def by_group(ap):
                return ap.rearrange("p (g i) k -> p g i k", g=G)

            for t in range(NT + 4):
                if 3 <= t < NT + 3:
                    normalise(t - 3)
                if t >= 4:
                    residual(t - 4)
                if t >= 5:
                    stats_2(t - 5)
                if t < NT:
                    u = t % 2
                    dve.wait_ge(s["score_s"], t + 1)
                    dve.tensor_reduce(top[:, u, :].rearrange("p (g i) -> p g i", g=G), score_view, AX_X, ALU.max)\
                        .then_inc(s["max_s"], 1)
                    dve.wait_ge(s["max_s"], t + 1)
                    if t >= 2:
                        dve.wait_ge(s["exp_s"], t - 1)
                    dve.tensor_tensor(by_group(shifted[:, u]), score_view,
                                      by_group(top[:, u, :].rearrange("p (h a) -> p h a", a=1).to_broadcast([P, H, S2])),
                                      ALU.subtract).then_inc(s["shift_s"], 1)
                if 1 <= t < NT + 1:
                    soft_sum(t - 1)
            stats_2(NT - 1)

            for t in range(NT):
                dve.wait_ge(s["st2_s"], t + 1)
                dve.bn_aggr(meanvar2[:, t, :], stats2[:, t, :]).then_inc(s["mv2_s"], 1)
            dve.wait_ge(s["mv2_s"], NT)
            dve.tensor_scalar(veps2[:], meanvar2[:, :, 1], EPS, None, ALU.add).then_inc(s["ve2_s"], 1)
            dve.wait_ge(s["rs2_s"], 1)
            step(dve.tensor_tensor(rr[:], rstd2[:], rstd2[:], ALU.mult))
            step(dve.tensor_tensor(rr[:], rr[:], meanvar2[:, :, 1], ALU.mult))
            dve.tensor_scalar(veps3[:], rr[:], EPS, None, ALU.add).then_inc(s["ve3_s"], 1)
            dve.wait_ge(s["ve3_s"], 1)
            dve.wait_ge(s["rs3_s"], 1)
            step(dve.tensor_tensor(rr[:], rstd2[:], rstd3[:], ALU.mult))
            for t in range(NT):
                dve.tensor_scalar(z2[:, t, :], x1[:, t, :], meanvar2[:, t, 0:1], rr[:, t:t + 1],
                                  ALU.subtract, ALU.mult).then_inc(s["z2_s"], 1)
            dve.wait_ge(s["iota_s"], 4)
            dve.tensor_copy(iota_f[:], iota_i[:])
            dve.tensor_copy(row_f[:], row_i[:])
            step(dve.tensor_copy(dump_f[:], dump_i[:]))

            dve.wait_ge(s["log_ps"], 1)
            step(dve.tensor_copy(logit[:], bank[2][:, 0:NT * E].rearrange("p (t e) -> p t e", t=NT)))
            for t in range(NT):
                m = dve.max(best[:, t, :], logit[:, t, :])
            step(m)
            for t in range(NT):
                m = dve.max_index(best_i[:, t, :], best[:, t, :], logit[:, t, :])
            dve.tensor_tensor(gap[:], best[:, :, 1], best[:, :, 0], ALU.subtract).then_inc(s["gap_s"], 1)
            step(m)
            step(dve.tensor_copy(choice_f[:], best_i[:, :, 0:TOPK].rearrange("p t k -> p k t")))
            for k in range(TOPK):
                m = dve.tensor_tensor(onehot[:, k], iota_f[:, 0:E].rearrange("p (a e) -> p a e", a=1)
                                      .to_broadcast([P, NT, E]),
                                      choice_f[:, k, :].rearrange("p (t a) -> p t a", a=1).to_broadcast([P, NT, E]),
                                      ALU.is_equal)
            step(m)
            dve.tensor_tensor(member[:], onehot[:, 0], onehot[:, 1], ALU.add).then_inc(s["member_s"], 1)

            for b in range(B):
                dve.wait_ge(s["shg_ps"], b + 1)
                dve.tensor_scalar(sh_gate[:, b * S:(b + 1) * S], bank[b], -10.0, 10.0, ALU.max, ALU.min)\
                    .then_inc(s["shc_s"], 1)

            dve.wait_ge(s["egap_s"], 1)
            step(dve.tensor_scalar(egap1[:], egap[:], 1.0, None, ALU.add))
            step(dve.reciprocal(wgt[:, 0, :], egap1[:]))
            step(dve.tensor_tensor(wgt[:, 1, :], wgt[:, 0, :], egap[:], ALU.mult))
            step(dve.tensor_scalar(wgt_g[:], wgt[:], tanh_g[:, 1:2], None, ALU.mult))
            step(dve.tensor_copy(w_hi[:], wgt_g[:].rearrange("p k t -> p (k t)")))

            dve.wait_ge(s["cnt_ps"], 1)
            step(dve.tensor_scalar(cnt_i[:], bank[6][:, 0:E], float(P - 1), None, ALU.add))
            step(dve.tensor_scalar(tiles_i[:], cnt_i[:], 7, None, ALU.logical_shift_right))
            step(dve.tensor_copy(tiles_f[:], tiles_i[:]))
            dve.wait_ge(s["const"], 7)
            step(dve.tensor_tensor(tiles_sq[:], upto[:], tiles_f[:].rearrange("p (a e) -> p a e", a=1)
                                   .to_broadcast([P, E, E]), ALU.mult))
            step(dve.tensor_reduce(tiles_incl[:], tiles_sq[:], AX_X, ALU.add))
            step(dve.tensor_tensor(tiles_excl[:], tiles_incl[:], tiles_f[:], ALU.subtract))
            step(dve.tensor_scalar(start[:], tiles_excl[:], float(P), None, ALU.mult))
            dve.wait_ge(s["rank_ps"], 1)
            step(dve.tensor_tensor(slot_te[:], bank[3][:, 0:NT * E].rearrange("p (t e) -> p t e", t=NT),
                                   start[:].rearrange("p (a e) -> p a e", a=1).to_broadcast([P, NT, E]), ALU.add))
            for k in range(TOPK):
                m = dve.tensor_tensor(slot_sel[:, k], onehot[:, k], slot_te[:], ALU.mult)
            step(m)
            step(dve.tensor_reduce(slot_f[:], slot_sel[:].rearrange("p k t e -> p (k t) e"), AX_X, ALU.add))
            step(dve.tensor_copy(slot_i[:], slot_f[:]))
            dve.tensor_scalar(sj_i[:], slot_i[:], 7, None, ALU.logical_shift_right)
            step(dve.tensor_scalar(sr_i[:], slot_i[:], P - 1, None, ALU.bitwise_and))
            dve.tensor_copy(sj_f[:], sj_i[:])
            step(dve.tensor_copy(sr_f[:], sr_i[:]))
            dve.tensor_copy(vals[:, :, 0], row_f[:])
            dve.memset(vals[:, :, 1], 1.0)
            dve.tensor_copy(vals[:, :, 2], w_hi[:].bitcast(F32))
            dve.tensor_tensor(vals[:, :, 3], wgt_g[:].rearrange("p k t -> p (k t)"), w_hi[:].bitcast(F32), ALU.subtract)
            dve.tensor_tensor(hot_r, iota_f[:].rearrange("p (a r) -> p a r", a=1).to_broadcast([P, PAIRS, P]),
                              sr_f[:].rearrange("p (n a) -> p n a", a=1).to_broadcast([P, PAIRS, P]), ALU.is_equal)\
                .then_inc(s["hotr_s"], 1)
            step(dve.tensor_tensor(hot_j[:], iota_f[:, 0:JC].rearrange("p (a j) -> p a j", a=1).to_broadcast([P, PAIRS, JC]),
                                   sj_f[:].rearrange("p (n a) -> p n a", a=1).to_broadcast([P, PAIRS, JC]), ALU.is_equal))
            dve.tensor_tensor(hot_v[:], hot_j[:].rearrange("p n (a j) -> p n a j", a=1).to_broadcast([P, PAIRS, 4, JC]),
                              vals[:].rearrange("p n (v a) -> p n v a", a=1).to_broadcast([P, PAIRS, 4, JC]), ALU.mult)\
                .then_inc(s["vals_s"], 1)
            step(dve.tensor_tensor(past[:], tiles_incl[:].rearrange("p (a e) -> p a e", a=1).to_broadcast([P, JC, E]),
                                   iota_f[:, 0:JC].rearrange("p (j a) -> p j a", a=1).to_broadcast([P, JC, E]),
                                   ALU.is_le))
            step(dve.tensor_reduce(exp_f[:], past[:], AX_X, ALU.add))
            step(dve.tensor_scalar(exp_c[:], exp_f[:], float(E - 1), None, ALU.min))
            dve.tensor_copy(exp_i[:], exp_c[:]).then_inc(s["expert_s"], 1)
            dve.wait_ge(s["list_ps"], 1)
            step(dve.tensor_copy(row_l[:], bank[7][:, 0:JC]))
            dve.tensor_tensor(used[:], bank[7][:, JC:2 * JC], dump_f[:], ALU.mult)
            step(dve.tensor_copy(row_li[:], row_l[:]))
            dve.tensor_scalar(gidx[:], row_li[:], TOK - 1, None, ALU.bitwise_and).then_inc(s["list_s"], 1)
            step(dve.tensor_tensor(used[:], dump_f[:], used[:], ALU.subtract))
            dve.tensor_tensor(sidx[:], row_l[:], used[:], ALU.add).then_inc(s["list_s"], 1)
            step(dve.tensor_copy(wslot[:], bank[7][:, 2 * JC:3 * JC]))
            dve.tensor_tensor(wslot[:], bank[7][:, 3 * JC:4 * JC], wslot[:], ALU.add).then_inc(s["list_s"], 1)

            for b in range(B):
                c = slice(b * S, (b + 1) * S)
                dve.wait_ge(s["shsilu_s"], b + 1)
                dve.tensor_tensor(sh_hT[:, c], bank[4 + b], sh_silu[:, c], ALU.mult).then_inc(s["shh_s"], 1)
            for t in range(NT):
                b = t // TPB
                dve.wait_ge(s["shd_ps"], b + 1)
                dve.scalar_tensor_tensor(out=base[:, t, :], in0=bank[b][:, (t % TPB) * D:(t % TPB + 1) * D],
                                         scalar=tanh_g[:, 1:2], in1=x1[:, t, :], op0=ALU.mult, op1=ALU.add)\
                    .then_inc(s["base_s"], 1)

            def rows_copy(j, u):
                dve.wait_ge(s["xgT_ps"], j + 1)
                if not isinstance(j, int) or j > 1:
                    dve.wait_ge(s["gu_ps"], (j - 1) * 2)
                dve.tensor_scalar(xgT[:, u], bank[0][:, 0:P], col_sb[:, 0:1], col_sb[:, 1:2], ALU.mult, ALU.add)\
                    .then_inc(s["xgT_s"], 1)

            def clip_tile(j, u):
                dve.wait_ge(s["gu_ps"], j * 2 + 1)
                if not isinstance(j, int) or j > 1:
                    dve.wait_ge(s["silu_s"], j - 1)
                dve.tensor_scalar(gate[:, u], bank[2 + u], -10.0, 10.0, ALU.max, ALU.min).then_inc(s["clip_s"], 1)

            def hid_tile(j, u):
                dve.wait_ge(s["silu_s"], j + 1)
                dve.wait_ge(s["gu_ps"], j * 2 + 2)
                if not isinstance(j, int) or j > 1:
                    dve.wait_ge(s["hT_ps"], j - 1)
                dve.tensor_tensor(hid[:, u], bank[4 + u], silu[:, u], ALU.mult).then_inc(s["hid_s"], 1)

            rows_copy(0, 0)
            rows_copy(1, 1)
            clip_tile(0, 0)
            hid_tile(0, 0)
            rows_copy(2, 0)
            clip_tile(1, 1)
            hid_tile(1, 1)
            with dve.Fori(0, (SLOT_TILES - 3) // 2) as i:
                for v in range(2):
                    rows_copy(i * 2 + (3 + v), (3 + v) % 2)
                    clip_tile(i * 2 + (2 + v), v % 2)
                    hid_tile(i * 2 + (2 + v), v % 2)
            clip_tile(SLOT_TILES - 1, 0)
            hid_tile(SLOT_TILES - 1, 0)

            dve.wait_ge(s["chosen_s"], 16)
            dve.tensor_tensor(sum1[:], base[:], chosen[:, 0], ALU.add).then_inc(s["sum1_s"], 1)
            dve.wait_ge(s["sum1_s"], 1)
            dve.tensor_tensor(result[:], sum1[:], chosen[:, 1], ALU.add).then_inc(s["result_s"], 1)


_INS = ['x', 'ctx_1024', 'fside_BxSxS2_0', 'mask_BxSxS2_ik1', 'g_xattn', 'g_ffn', 'L0_xattn_wq_k', 'L0_xattn_wq_b',
        'L0_xattn_wk_k', 'L0_xattn_wk_b', 'L0_xattn_wv_k', 'L0_xattn_wv_b', 'L0_xattn_wo_k', 'L0_xattn_wo_b',
        'L0_ffn_ln_gamma', 'L0_ffn_ln_beta', 'L0_ffn_router_w', 'L0_ffn_gate_up_w', 'L0_ffn_down_w',
        'L0_ffn_shared_gate_up_w', 'L0_ffn_shared_down_w']


def kernel(**inputs):
    import numpy as _np
    import concourse.bacc as _bacc
    from concourse import mybir as _mybir
    from concourse.bass_utils import run_bass_kernel_spmd as _run

    nc = _bacc.Bacc("TRN2", target_bir_lowering=False, num_devices=1)
    arrays, args = {}, []
    for name in _INS:
        a = _np.ascontiguousarray(inputs[name])
        arrays[f"in_{name}_dram"] = a
        args.append(nc.dram_tensor(f"in_{name}_dram", a.shape, _mybir.dt.from_np(a.dtype), kind="ExternalInput").ap())
    shape = inputs["x"].shape
    args.append(nc.dram_tensor("out_0_dram", shape, _mybir.dt.float32, kind="ExternalOutput").ap())
    gated_block(nc, *args)
    r = _run(nc, [arrays], core_ids=[0])
    return r.results[0]["out_0_dram"]
```

```python
from contextlib import ExitStack

import concourse.bass as bass
from concourse import mybir

ALU = mybir.AluOpType
ACT = mybir.ActivationFunctionType
F32 = mybir.dt.float32
F32R = mybir.dt.float32r
BF16 = mybir.dt.bfloat16
I32 = mybir.dt.int32
U32 = mybir.dt.uint32
AX_X = mybir.AxisListType.X


def gated_block(nc, x, ctx_in, group_prob, mask, g_xattn, g_ffn, wq, bq, wk, bk, wv, bv, wo, bo,
                ln_gamma, ln_beta, router_w, gate_up_w, down_w, sh_gate_up_w, sh_down_w, out):
    P = 128
    B, S, D = x.shape
    S2 = ctx_in.shape[1]
    KP = S2 + S2 % 2
    H, DH = 16, D // 16
    G = 4
    HG = H // G
    TPB = S // P
    NT = B * TPB
    TOK = B * S
    E, F = down_w.shape[0], down_w.shape[1]
    FS = sh_down_w.shape[0]
    FC = F // P
    TOPK = 2
    PAIRS = TOPK * NT
    SLOT_TILES = TOK * TOPK // P + E - 1
    JC = SLOT_TILES + SLOT_TILES % 2
    EPS = 1e-5
    RING = 4
    NV = 2
    SP = 3 * P // G
    QU = 2 * P
    QSCALE = float(DH) ** -0.5
    assert D == P and FS == P and H == G * HG and HG * KP <= 512

    x_tiles, gp_tiles, mask_tiles, out_tiles = ([a[b].rearrange("(p t) d -> p t d", p=P) for b in range(B)]
                                                for a in (x, group_prob, mask, out))
    normed_dram = nc.dram_tensor("normed_rows", (TOK, D), F32, kind="Internal").ap()
    chosen_dram = nc.dram_tensor("chosen_rows", (TOPK * TOK + SLOT_TILES * P, D), F32, kind="Internal").ap()

    with ExitStack() as ctx:
        def sb(name, shape, dt=F32):
            return ctx.enter_context(nc.sbuf_tensor(name, shape, dt))

        attention = ExitStack()

        def at(name, shape, dt=F32):
            return attention.enter_context(nc.sbuf_tensor(name, shape, dt))

        def sem(name):
            return ctx.enter_context(nc.semaphore(name))

        quad = ctx.enter_context(nc.psum_tensor("banks0to3", [P, 4, 512], F32))
        bank = [quad[:, i, :] for i in range(4)] + \
            [ctx.enter_context(nc.psum_tensor(f"bank{i}", [P, 512], F32))[:] for i in range(4, 8)]

        x_sb = sb("x_sb", [P, NT, D])
        wo_sb = sb("wo_sb", [P, D])
        col_sb = sb("col_sb", [P, 2])
        gates_sb = sb("gates_sb", [P, 2])
        router_sb = sb("router_sb", [P, E])
        gu_low = sb("gu_low", [P, E * 2 * F], F32R)
        gu_high = sb("gu_high", [P, E * 2 * F], F32R)
        down_sb = sb("down_sb", [P, E * FC * D])
        shgu_sb = sb("shgu_sb", [P, 2 * FS])
        shdown_sb = sb("shdown_sb", [P, D])
        ident = sb("ident", [P, P])
        ident_r = sb("ident_r", [P, P], F32R)
        earlier = sb("earlier", [P, P], BF16)
        ones = sb("ones", [P, P], BF16)
        upto = sb("upto", [P, E, E])
        iota_i = sb("iota_i", [P, P], I32)
        iota_f = sb("iota_f", [P, P])
        iota_b = sb("iota_b", [P, P], BF16)
        part_col = sb("part_col", [P, PAIRS], I32)
        tile_row = sb("tile_row", [P, PAIRS], I32)
        dump_i = sb("dump_i", [P, JC], I32)
        dump_f = sb("dump_f", [P, JC])
        neghalf = sb("neghalf", [P, NT])
        z_sb = sb("z_sb", [P, NT, D])
        xb = x_sb
        zT = sb("zT", [P, TOK])
        tanh_g = sb("tanh_g", [P, 2])
        x1 = sb("x1", [P, NT, D])

        gp_sb = at("gp_sb", [P, NT, S2])
        mask_sb = at("mask_sb", [P, NT, S2], I32)
        wq_sb, wv_sb = (at(n, [P, D]) for n in ("wq_sb", "wv_sb"))
        wq3 = at("wq3", [P, G, 3, P // G])
        bq_sb = at("bq_sb", [SP, G])
        bk_sb = at("bk_sb", [SP, G])
        bkq = at("bkq", [SP, G])
        bv_sb = at("bv_sb", [S2, D])
        bo_sb = at("bo_sb", [P, D])
        part_i = at("part_i", [SP, HG], I32)
        part_b = at("part_b", [SP, HG], I32)
        headsel = at("headsel", [SP, HG])
        stats = at("stats", [P, NT, 6])
        meanvar = at("meanvar", [P, NT, 2])
        veps = at("veps", [P, NT])
        rstd = at("rstd", [P, NT])
        q_stack = at("q_stack", [SP, G, TOK], F32R)
        ctxT = at("ctxT", [P, B, S2])
        k_stack = at("k_stack", [SP, G, B, HG, KP], F32R)
        v_pad = at("v_pad", [S2, B, G, HG, HG, DH])
        neg = at("neg", [P, NT, S2])
        neg_hi = at("neg_hi", [P, NT, KP], F32R)
        neg_lo = at("neg_lo", [P, NT, KP], F32R)
        bo_g = at("bo_g", [P, D])
        top = at("top", [P, 2, H])
        prob = at("prob", [P, 2, H, S2])
        probT = at("probT", [P, 2, HG, G, P])
        sums = at("sums", [P, 2, H])
        rsum = at("rsum", [P, 2, H])
        rsum_wide = at("rsum_wide", [P, 2, H, DH])
        rsumT = at("rsumT", [P, 2, P])
        attT = at("attT", [P, 2, P])
        start_up = ExitStack()

        def early(name, shape, dt=F32):
            return start_up.enter_context(nc.sbuf_tensor(name, shape, dt))

        ctx_sb = early("ctx_sb", [S2, B, D])
        wk_sb = early("wk_sb", [P, D])
        wk3 = early("wk3", [P, G, 3, P // G])
        k_full = early("k_full", [SP, G, B, S2])
        k_hi = early("k_hi", [SP, G, B, S2], F32R)
        start_up.close()
        shifted = at("shifted", [P, 2, H, S2])
        attention.close()

        stats2 = sb("stats2", [P, NT, 6])
        meanvar2 = sb("meanvar2", [P, NT, 2])
        veps2 = sb("veps2", [P, NT])
        rr = sb("rr", [P, NT])
        z2 = z_sb
        x2T = zT
        logit = sb("logit", [P, NT, E])
        best = sb("best", [P, NT, 8])
        best_i = sb("best_i", [P, NT, 8], U32)
        choice_f = sb("choice_f", [P, TOPK, NT])
        onehot = sb("onehot", [P, TOPK, NT, E])
        member = sb("member", [P, NT, E], BF16)
        gap = sb("gap", [P, NT])
        egap = sb("egap", [P, NT])
        egap1 = sb("egap1", [P, NT])
        wgt = sb("wgt", [P, TOPK, NT])
        wgt_g = sb("wgt_g", [P, TOPK, NT])
        cnt_i = sb("cnt_i", [P, E], I32)
        tiles_i = sb("tiles_i", [P, E], I32)
        tiles_f = sb("tiles_f", [P, E])
        tiles_sq = sb("tiles_sq", [P, E, E])
        tiles_incl = sb("tiles_incl", [P, E])
        tiles_excl = sb("tiles_excl", [P, E])
        rank_te = sb("rank_te", [P, PAIRS, E])
        rank_f = sb("rank_f", [P, PAIRS])
        rank_i = sb("rank_i", [P, PAIRS], I32)
        first_te = sb("first_te", [P, PAIRS, E])
        first_f = sb("first_f", [P, PAIRS])
        nth_i = sb("nth_i", [P, PAIRS], I32)
        nth_f = sb("nth_f", [P, PAIRS])
        row_i = sb("row_i", [P, PAIRS], I32)
        sj_b = sb("sj_b", [P, PAIRS], BF16)
        sr_b = sb("sr_b", [P, PAIRS], BF16)
        hot_r = sb("hot_r", [P, PAIRS, P], BF16)
        hot_j = sb("hot_j", [P, PAIRS, JC], BF16)
        part_f = sb("part_f", [P, 1])
        tile_row_b = sb("tile_row_b", [P, PAIRS], BF16)
        hot_v = sb("hot_v", [P, PAIRS, NV, JC], BF16)
        lists = sb("lists", [P, NV, JC])
        row_li = sb("row_li", [P, JC], I32)
        unused = sb("unused", [P, JC])
        gidx = sb("gidx", [P, JC], I32)
        sidx = sb("sidx", [P, JC], I32)
        past = sb("past", [P, JC, E])
        exp_f = sb("exp_f", [P, JC])
        exp_c = sb("exp_c", [P, JC])
        exp_i = sb("exp_i", [P, JC], I32)

        sh_gate = sb("sh_gate", [P, TOK])
        sh_silu = sb("sh_silu", [P, TOK])
        sh_hT = sb("sh_hT", [P, TOK])
        base = sb("base", [P, NT, D])

        xg = sb("xg", [P, RING, D])
        xgT = sb("xgT", [P, 2, P])
        xgT_hi = sb("xgT_hi", [P, 2, P], F32R)
        xgT_lo = sb("xgT_lo", [P, 2, P], F32R)
        gate = sb("gate", [P, 2, F])
        silu = sb("silu", [P, 2, F])
        hid = sb("hid", [P, 2, F])
        hidT = sb("hidT", [P, 2, F])
        y_all = sb("y_all", [P, SLOT_TILES, D])
        chosen = sb("chosen", [P, TOPK, NT, D])
        sum1 = x_sb
        shared = sb("shared", [P, TOK])
        result = z2

        def columns(e):
            return slice(e * 2 * F, (e + 1) * 2 * F)

        names = """x_in0 x_in1 ctx_in k_in v_in q_in col_in bk_in bq_in gp_in mask_in0 mask_in1 small_in sh_in
            gate_in whigh_s wlow_s down_in const iota_s headsel_s ident_s identr_s stats_s mv_s veps_s
            rstd_s z_s0 z_s1 zT_ps zT_sb q_ps qhi_s qlo_s ctxT_ps ctxT_sb wq3_s wk3_s k_ps bkq_s kf_s khi_s
            klo_s ks_s0 ks_s1 kz_s v_ps vz_s v_s neg_s0 neg_s1 neg_s negz_s tanh_s bog_s xb_s score_s max_s
            shift_s exp_s prob_s pt_ps pt_sb o_ps r_ps r_sb sum_s rsum_s rwide_s att_s y_ps x1_s st2_s mv2_s
            ve2_s rr_s z2_s z2_out x2_ps x2_s log_ps dstep gap_s egap_s partf_s member_s rank_ps cnt_ps
            hotj_s hotr_s hotv_s0 hotv_s1 list_ps list_s expert_s shg_ps shu_ps shc_s shsilu_s shh_s shd_ps
            base_s xg_s0 xg_s1 xg_s2 xg_s3 xgT_ps xf_s xh_s xgT_s gu_ps clip_s silu_s hid_s hT_ps hT_s yy_ps
            yy_s scat_s shared_s chosen_s00 chosen_s01 chosen_s10 chosen_s11 sum1_s wgt_s second_s result_s
            out_s""".split() + \
            [f"gu_in{e}" for e in range(E)]
        s = {n: sem(n) for n in names}

        block = ctx.enter_context(nc.Block())

        def normalised(engine, b):
            engine.wait_ge(s["rstd_s"], b + 1)
            engine.wait_ge(s["mv_s"], TPB * (b + 1))
            engine.wait_ge(s[f"x_in{b}"], 16)
            for t in range(b * TPB, (b + 1) * TPB):
                engine.tensor_scalar(z_sb[:, t, :], x_sb[:, t, :], meanvar[:, t, 0:1], rstd[:, t:t + 1],
                                     ALU.subtract, ALU.mult).then_inc(s[f"z_s{b}"], 1)

        HEAD, UNROLL = RING, 2 * RING
        ROUNDS = (SLOT_TILES - 2 - HEAD) // UNROLL
        assert HEAD % RING == 0 and UNROLL % RING == 0

        def pipeline(engine, step):
            for j in range(-2, HEAD):
                step(j, j % RING, j // RING)
            with engine.Fori(0, ROUNDS) as i:
                for v in range(UNROLL):
                    step(i * UNROLL + (HEAD + v), v % RING, i * (UNROLL // RING) + (HEAD + v) // RING)
            for j in range(HEAD + UNROLL * ROUNDS, SLOT_TILES + 3):
                step(j, j % RING, j // RING)

        def exists(j, ahead):
            return not isinstance(j, int) or 0 <= j + ahead < SLOT_TILES

        @block.sync
        def _(sp):
            sp.dma_start(x_sb[:, 0:TPB, :], x_tiles[0]).then_inc(s["x_in0"], 16)
            sp.dma_start(wq_sb[:], wq).then_inc(s["q_in"], 16)
            sp.dma_start(x_sb[:, TPB:NT, :], x_tiles[1]).then_inc(s["x_in1"], 16)
            sp.dma_start(wv_sb[:], wv).then_inc(s["v_in"], 16)
            sp.dma_start(bv_sb[:], bv.rearrange("(a d) -> a d", a=1).to_broadcast([S2, D])).then_inc(s["v_in"], 16)
            for dst, v, name in ((bk_sb, bk, "bk_in"), (bq_sb, bq, "bq_in")):
                for a in range(3):
                    with nc.allow_non_contiguous_dma(reason="a bias on the partitions of its rows"):
                        sp.dma_start(dst[32 * a:32 * a + 32, :], v.rearrange("(g r) -> r g", g=G))\
                            .then_inc(s[name], 16)
            for b in range(B):
                sp.dma_start(mask_sb[:, b * TPB:(b + 1) * TPB, :], mask_tiles[b])\
                    .then_inc(s[f"mask_in{b}"], 16)
            sp.dma_start(gates_sb[:, 0:1], g_xattn.rearrange("(a d) -> a d", a=1).to_broadcast([P, 1]))\
                .then_inc(s["gate_in"], 16)
            sp.dma_start(gates_sb[:, 1:2], g_ffn.rearrange("(a d) -> a d", a=1).to_broadcast([P, 1]))\
                .then_inc(s["gate_in"], 16)
            sp.dma_start(bo_sb[:], bo.rearrange("(a d) -> a d", a=1).to_broadcast([P, D])).then_inc(s["gate_in"], 16)
            for b in range(B):
                sp.dma_start(gp_sb[:, b * TPB:(b + 1) * TPB, :], gp_tiles[b]).then_inc(s["gp_in"], 16)
            sp.dma_start(wo_sb[:], wo).then_inc(s["small_in"], 16)
            sp.dma_start(router_sb[:], router_w).then_inc(s["small_in"], 16)
            for n, v in enumerate((ln_gamma, ln_beta)):
                sp.dma_start(col_sb[:, n:n + 1], v.rearrange("(d a) -> d a", a=1)).then_inc(s["col_in"], 16)
            sp.dma_start(shgu_sb[:], sh_gate_up_w).then_inc(s["sh_in"], 16)
            sp.dma_start(shdown_sb[:], sh_down_w).then_inc(s["sh_in"], 16)
            for e in range(E):
                sp.dma_start(gu_low[:, e * 2 * F:(e + 1) * 2 * F].bitcast(F32), gate_up_w[e]).then_inc(s[f"gu_in{e}"], 16)
            for e in range(E):
                sp.dma_start(down_sb[:, e * FC * D:(e + 1) * FC * D].rearrange("p (c d) -> p c d", c=FC),
                             down_w[e].rearrange("(c p) d -> p c d", p=P)).then_inc(s["down_in"], 16)
            for b in range(B):
                half = slice(b * TPB, (b + 1) * TPB)
                sp.wait_ge(s["z2_s"], TPB * (b + 1))
                sp.dma_start(normed_dram.rearrange("(t p) d -> p t d", p=P)[:, half], z2[:, half]).then_inc(s["z2_out"], 16)
            sp.wait_ge(s["scat_s"], 16 * SLOT_TILES)
            chosen_rows = chosen_dram[0:TOPK * TOK, :].rearrange("(k t p) d -> p k t d", k=TOPK, p=P)
            for b in range(B):
                half = slice(b * TPB, (b + 1) * TPB)
                for k in range(TOPK):
                    sp.dma_start(chosen[:, k, half], chosen_rows[:, k, half]).then_inc(s[f"chosen_s{b}{k}"], 16)
            for b in range(B):
                half = slice(b * TPB, (b + 1) * TPB)
                sp.wait_ge(s["result_s"], b + 1)
                sp.dma_start(out_tiles[b], result[:, half]).then_inc(s["out_s"], 16)
            sp.wait_ge(s["out_s"], 16 * B)

        @block.gpsimd
        def _(pool):
            pool.memset(neghalf[:], -0.5).then_inc(s["const"], 1)
            pool.memset(ident[:], 0.0).then_inc(s["const"], 1)
            pool.wait_ge(s["const"], 2)
            pool.affine_select(out=ident[:], in_=ident[:], compare_op=ALU.not_equal, fill=1.0, base=0,
                               pattern=[[-1, P]], channel_multiplier=1).then_inc(s["ident_s"], 1)
            pool.iota(part_i[:], [[0, HG]], base=0, channel_multiplier=1).then_inc(s["iota_s"], 1)
            pool.iota(iota_i[:], [[1, P]], base=0, channel_multiplier=0).then_inc(s["iota_s"], 1)
            pool.wait_ge(s["ident_s"], 1)
            pool.tensor_copy(ident_r[:], ident[:]).then_inc(s["identr_s"], 1)
            for b in range(B):
                half = slice(b * TPB, (b + 1) * TPB)
                pool.wait_ge(s["veps_s"], b + 1)
                pool.tensor_tensor(rstd[:, half], veps[:, half], neghalf[:, half], ALU.pow).then_inc(s["rstd_s"], 1)

            def mask_term(b):
                half = slice(b * TPB, (b + 1) * TPB)
                pool.wait_ge(s[f"mask_in{b}"], 16)
                pool.tensor_scalar(neg[:, half], mask_sb[:, half], -1.0, 1e9, ALU.add, ALU.mult).then_inc(s["neg_s"], 1)
                pool.wait_ge(s["neg_s"], b + 1)
                pool.tensor_copy(neg_hi[:, half, 0:S2], neg[:, half]).then_inc(s[f"neg_s{b}"], 1)
                pool.wait_ge(s[f"neg_s{b}"], 1)
                pool.tensor_tensor(neg_lo[:, half, 0:S2], neg[:, half], neg_hi[:, half, 0:S2].bitcast(F32),
                                   ALU.subtract).then_inc(s[f"neg_s{b}"], 1)

            mask_term(0)
            pool.wait_ge(s["klo_s"], 1)
            pool.wait_ge(s["kf_s"], G)
            pool.wait_ge(s["headsel_s"], 1)
            for g in range(G):
                pool.tensor_tensor(k_stack[:, g, 1, :, 0:S2], k_full[:, g, 1:2, :].to_broadcast([SP, HG, S2]),
                                   headsel[:].rearrange("p (i a) -> p i a", a=1).to_broadcast([SP, HG, S2]),
                                   ALU.mult).then_inc(s["ks_s1"], 1)
            pool.iota(part_col[:], [[0, PAIRS]], base=0, channel_multiplier=1).then_inc(s["iota_s"], 1)
            pool.iota(tile_row[:], [[TOK, TOPK], [P, NT]], base=TOPK * TOK, channel_multiplier=0).then_inc(s["iota_s"], 1)
            pool.iota(dump_i[:], [[P, JC]], base=2 * TOPK * TOK, channel_multiplier=1).then_inc(s["iota_s"], 1)
            pool.memset(ones[:], 1.0).then_inc(s["const"], 1)
            pool.memset(earlier[:], 1.0).then_inc(s["const"], 1)
            pool.memset(upto[:], 1.0).then_inc(s["const"], 1)
            pool.wait_ge(s["const"], 5)
            pool.affine_select(out=earlier[:], in_=earlier[:], compare_op=ALU.is_gt, fill=0.0, base=0,
                               pattern=[[1, P]], channel_multiplier=-1).then_inc(s["const"], 1)
            pool.affine_select(out=upto[:], in_=upto[:], compare_op=ALU.is_ge, fill=0.0, base=0,
                               pattern=[[1, E], [-1, E]], channel_multiplier=0).then_inc(s["const"], 1)
            mask_term(1)
            assert E == NT

            def weights_low(n):
                pool.wait_ge(s["whigh_s"], 2 * (n + 1))
                pool.tensor_tensor(gu_low[:, columns(n)], gu_low[:, columns(n)].bitcast(F32),
                                   gu_high[:, columns(n)].bitcast(F32), ALU.subtract).then_inc(s["wlow_s"], 1)

            pool.wait_ge(s["gp_in"], 16 * B)
            for t in range(NT):
                u = t % 2
                pool.wait_ge(s["exp_s"], t + 1)
                if t >= 2:
                    pool.wait_ge(s["pt_ps"], HG * (t - 1))
                pool.tensor_tensor(prob[:, u], shifted[:, u], gp_sb[:, t:t + 1, :].to_broadcast([P, H, S2]),
                                   ALU.mult).then_inc(s["prob_s"], 1)
                weights_low(t)
                if t == 1:
                    pool.wait_ge(s["bog_s"], 1)
                    pool.wait_ge(s["x_in0"], 16)
                    pool.wait_ge(s["x_in1"], 16)
                    pool.tensor_tensor(xb[:], x_sb[:], bo_g[:].rearrange("p (a d) -> p a d", a=1).to_broadcast([P, NT, D]),
                                       ALU.add).then_inc(s["xb_s"], 1)
            for b in range(B):
                half = slice(b * TPB, (b + 1) * TPB)
                pool.wait_ge(s["ve2_s"], b + 1)
                pool.tensor_tensor(rr[:, half], veps2[:, half], neghalf[:, half], ALU.pow).then_inc(s["rr_s"], 1)

            pool.wait_ge(s["partf_s"], 1)
            pool.wait_ge(s["hotj_s"], 1)
            pool.tensor_tensor(hot_v[:, :, 1, :], hot_j[:], tile_row_b[:].rearrange("p (n a) -> p n a", a=1)
                               .to_broadcast([P, PAIRS, JC]), ALU.mult).then_inc(s["hotv_s1"], 1)

            pool.wait_ge(s["z2_out"], 16 * B)
            pool.wait_ge(s["list_s"], 1)

            def gather(j):
                if j >= RING:
                    pool.wait_ge(s["xgT_ps"], j - RING + 1)
                pool.indirect_dma_start(xg[:, j % RING, :], None, normed_dram,
                                        bass.IndirectOffsetOnAxis(ap=gidx[:, j:j + 1], axis=0))\
                    .then_inc(s[f"xg_s{j % RING}"], 16)

            def scatter(j):
                pool.wait_ge(s["yy_s"], j + 1)
                if j == 0:
                    pool.wait_ge(s["list_s"], 2)
                pool.indirect_dma_start(chosen_dram, bass.IndirectOffsetOnAxis(ap=sidx[:, j:j + 1], axis=0),
                                        y_all[:, j, :], None).then_inc(s["scat_s"], 16)

            LAG = 8
            for j in range(SLOT_TILES):
                gather(j)
                if j == SLOT_TILES // 2:
                    pool.wait_ge(s["shared_s"], B)
                    pool.wait_ge(s["x1_s"], NT)
                    pool.tensor_tensor(base[:], shared[:].rearrange("p (t d) -> p t d", t=NT), x1[:], ALU.add)\
                        .then_inc(s["base_s"], 1)
                if j >= LAG:
                    scatter(j - LAG)
            for j in range(SLOT_TILES - LAG, SLOT_TILES):
                scatter(j)

        @block.scalar
        def _(act):
            act.dma_start(ctx_sb[:], ctx_in.rearrange("b k d -> k b d")).then_inc(s["ctx_in"], 16)
            act.dma_start(wk_sb[:], wk).then_inc(s["k_in"], 16)

            def evac(dst, src):
                return act.activation(dst, src, ACT.Copy)

            def thrice(dst, src):
                return act.activation(dst[:], src[:].rearrange("p (g a r) -> p g a r", g=G, a=1)
                                      .to_broadcast([P, G, 3, P // G]), ACT.Copy)

            act.wait_ge(s["k_in"], 16)
            thrice(wk3, wk_sb).then_inc(s["wk3_s"], 1)
            act.wait_ge(s["ctxT_ps"], 1)
            evac(ctxT[:], bank[7][:, 0:B * S2].rearrange("p (b k) -> p b k", b=B)).then_inc(s["ctxT_sb"], 1)
            act.wait_ge(s["q_in"], 16)
            thrice(wq3, wq_sb).then_inc(s["wq3_s"], 1)
            act.wait_ge(s["bkq_s"], 1)
            act.wait_ge(s["k_ps"], 1)
            for g in range(G):
                act.activation(k_full[:, g], bank[2 + g // 2][0:SP, (g % 2) * B * S2:(g % 2 + 1) * B * S2]
                               .rearrange("p (b k) -> p b k", b=B), ACT.Identity, bias=bkq[:, g:g + 1], scale=QSCALE)\
                    .then_inc(s["kf_s"], 1)
            act.wait_ge(s["zT_ps"], 1)
            evac(zT[:, 0:S], bank[0]).then_inc(s["zT_sb"], 1)

            def q_round(n):
                for g in range(G):
                    act.wait_ge(s["q_ps"], n * G + g + 1)
                    act.activation(q_stack[:, g, n * QU:(n + 1) * QU], bank[4 + g][0:SP, 0:QU],
                                   ACT.Identity, bias=bq_sb[:, g:g + 1]).then_inc(s["qhi_s"], 1)

            act.wait_ge(s["bq_in"], 48)
            q_round(0)
            act.wait_ge(s["gate_in"], 48)
            act.activation(tanh_g[:], gates_sb[:], ACT.Tanh).then_inc(s["tanh_s"], 1)

            def weights_high(n, half):
                act.wait_ge(s[f"gu_in{n}"], 16)
                part = slice((2 * n + half) * F, (2 * n + half + 1) * F)
                evac(gu_high[:, part], gu_low[:, part].bitcast(F32)).then_inc(s["whigh_s"], 1)

            def exp_tile(t):
                u = t % 2
                act.wait_ge(s["shift_s"], t + 1)
                act.activation(shifted[:, u], shifted[:, u], ACT.Exp).then_inc(s["exp_s"], 1)

            def back_tile(t):
                u = t % 2
                for i in range(HG):
                    act.wait_ge(s["pt_ps"], HG * t + i + 1)
                    if i == 0 and t >= 2:
                        act.wait_ge(s["o_ps"], t - 1)
                    evac(probT[0:S2, u, i], bank[4 + i % 2][0:S2, :].rearrange("p (g q) -> p g q", g=G))\
                        .then_inc(s["pt_sb"], 1)
                    if i == 1 and t + 2 < NT:
                        weights_high(t + 2, 0)
                if t + 2 < NT:
                    exp_tile(t + 2)
                    weights_high(t + 2, 1)
                act.wait_ge(s["r_ps"], t + 1)
                if t >= 2:
                    act.wait_ge(s["att_s"], t - 1)
                evac(rsumT[:, u], bank[6 + u][:, P:2 * P]).then_inc(s["r_sb"], 1)

            for t in range(NT + 2):
                if t == 0:
                    act.wait_ge(s["zT_ps"], 2)
                    evac(zT[:, S:2 * S], bank[4]).then_inc(s["zT_sb"], 1)
                if t < 3:
                    q_round(t + 1)
                if t >= 2:
                    back_tile(t - 2)
                elif t < NT:
                    exp_tile(t)
                    weights_high(t, 0)
                    weights_high(t, 1)

            act.wait_ge(s["col_in"], 32)
            for b in range(B):
                act.wait_ge(s["x2_ps"], b + 1)
                act.activation(x2T[:, b * S:(b + 1) * S], bank[b], ACT.Identity, bias=col_sb[:, 1:2],
                               scale=col_sb[:, 0:1]).then_inc(s["x2_s"], 1)
            act.wait_ge(s["gap_s"], B)
            act.activation(egap[:], gap[:], ACT.Exp).then_inc(s["egap_s"], 1)
            act.wait_ge(s["partf_s"], 1)
            act.wait_ge(s["hotj_s"], 1)
            act.activation(hot_v[:, :, 0, :], hot_j[:], ACT.Copy, scale=part_f[:]).then_inc(s["hotv_s0"], 1)
            for b in range(B):
                act.wait_ge(s["shc_s"], b + 1)
                act.activation(sh_silu[:, b * S:(b + 1) * S], sh_gate[:, b * S:(b + 1) * S], ACT.Silu)\
                    .then_inc(s["shsilu_s"], 1)

            def rows_high(j, u):
                act.wait_ge(s["xf_s"], j + 1)
                if not isinstance(j, int) or j > 1:
                    act.wait_ge(s["gu_ps"], (j - 1) * 2)
                evac(xgT_hi[:, u], xgT[:, u]).then_inc(s["xh_s"], 1)

            def silu_tile(j, u):
                act.wait_ge(s["clip_s"], j + 1)
                act.activation(silu[:, u], gate[:, u], ACT.Silu).then_inc(s["silu_s"], 1)

            def hidden_copy(j, u):
                act.wait_ge(s["hT_ps"], j + 1)
                evac(hidT[:, u], bank[6]).then_inc(s["hT_s"], 1)

            def y_tile(j, u):
                act.wait_ge(s["yy_ps"], j + 1)
                evac(y_all[:, bass.ds(j, 1), :].rearrange("p a d -> p (a d)"), bank[7][:, 0:D]).then_inc(s["yy_s"], 1)

            def shared_tile(b):
                act.wait_ge(s["shd_ps"], b + 1)
                act.activation(shared[:, b * S:(b + 1) * S], bank[1], ACT.Copy, scale=tanh_g[:, 1:2])\
                    .then_inc(s["shared_s"], 1)

            def act_step(j, r, n):
                if exists(j, -2):
                    hidden_copy(j - 2, r % 2)
                if exists(j, -3):
                    y_tile(j - 3, (r + 1) % 2)
                if exists(j, 0):
                    silu_tile(j, r % 2)
                if exists(j, 2):
                    rows_high(j + 2, r % 2)
                if isinstance(j, int) and j == 0:
                    shared_tile(1)

            shared_tile(0)
            pipeline(act, act_step)

            act.wait_ge(s["wgt_s"], 1)
            for b in range(B):
                act.wait_ge(s[f"chosen_s{b}1"], 16)
                for t in range(b * TPB, (b + 1) * TPB):
                    act.activation(chosen[:, 1, t, :], chosen[:, 1, t, :], ACT.Copy, scale=wgt_g[:, 1, t:t + 1])\
                        .then_inc(s["second_s"], 1)

        @block.tensor
        def _(pe):
            pe.wait_ge(s["ident_s"], 1)
            pe.wait_ge(s["ctx_in"], 16)
            for b in range(B):
                m = pe.transpose(bank[7][:, b * S2:(b + 1) * S2], ctx_sb[:, b, :], ident[0:S2, 0:S2])
            m.then_inc(s["ctxT_ps"], 1)

            def rows_transposed(b):
                if b == 1:
                    pe.wait_ge(s["qlo_s"], 1)
                    pe.wait_ge(s["qhi_s"], 1)
                pe.wait_ge(s[f"z_s{b}"], TPB)
                for t in range(TPB):
                    m = pe.transpose(bank[4 * b][:, t * P:(t + 1) * P], z_sb[:, b * TPB + t, :], ident[:])
                m.then_inc(s["zT_ps"], 1)

            pe.wait_ge(s["ctxT_sb"], 1)
            pe.wait_ge(s["wk3_s"], 1)
            for g in range(G):
                m = pe.matmul(bank[2 + g // 2][0:SP, (g % 2) * B * S2:(g % 2 + 1) * B * S2],
                              wk3[:, g].rearrange("p a r -> p (a r)"),
                              ctxT[:].rearrange("p b k -> p (b k)"), start=True, stop=True)
            m.then_inc(s["k_ps"], 1)
            rows_transposed(0)

            def queries(n):
                if n == 0:
                    pe.wait_ge(s["wq3_s"], 1)
                for g in range(G):
                    if n >= 1:
                        pe.wait_ge(s["qlo_s"], (n - 1) * G + g + 1)
                        pe.wait_ge(s["qhi_s"], (n - 1) * G + g + 1)
                    if g == 0:
                        pe.wait_ge(s["zT_sb"], min(n, 1) + 1)
                    pe.matmul(bank[4 + g][0:SP, 0:QU],
                              wq3[:, g].rearrange("p a r -> p (a r)"),
                              zT[:, n * QU:(n + 1) * QU], start=True, stop=True).then_inc(s["q_ps"], 1)

            def values():
                pe.wait_ge(s["v_in"], 32)
                for b in range(B):
                    m = pe.matmul(bank[1][0:S2, b * D:(b + 1) * D], ctxT[:, b, :], wv_sb[:], start=True, stop=True)
                m.then_inc(s["v_ps"], 1)

            values()
            queries(0)

            def scores(t):
                b = t // TPB
                if t == 0:
                    pe.wait_ge(s["identr_s"], 1)
                    pe.wait_ge(s["negz_s"], 2)
                    pe.wait_ge(s["kz_s"], 1)
                    pe.wait_ge(s["kf_s"], G)
                    pe.wait_ge(s["zT_sb"], 1)
                    pe.wait_ge(s["v_s"], B * HG)
                if t % TPB == 0:
                    pe.wait_ge(s[f"neg_s{b}"], 2)
                    pe.wait_ge(s[f"ks_s{b}"], G)
                if t > 0:
                    pe.wait_ge(s["shift_s"], t)
                for g in range(G):
                    dst = bank[g][:, 0:HG * KP]
                    for n, part in enumerate((neg_hi, neg_lo)):
                        pe.matmul(dst, ident_r[:], part[:, t:t + 1, :].to_broadcast([P, HG, KP]),
                                  start=(n == 0), stop=False)
                    if t * P % QU == 0:
                        pe.wait_ge(s["qlo_s"], t * P // QU * G + g + 1)
                        pe.wait_ge(s["qhi_s"], t * P // QU * G + g + 1)
                    m = pe.matmul(dst, q_stack[:, g, t * P:(t + 1) * P],
                                  k_stack[:, g, b].rearrange("p i k -> p (i k)"), start=False, stop=True)
                m.then_inc(s["score_s"], 1)

            def attend(t):
                b, u = t // TPB, t % 2
                pe.wait_ge(s["prob_s"], t + 1)
                if t == 0:
                    pe.wait_ge(s["v_s"], B * HG)
                    pe.wait_ge(s["qlo_s"], TOK // QU * G)
                    pe.wait_ge(s["qhi_s"], TOK // QU * G)

                def turn(i):
                    k = HG * t + i
                    if k >= 2:
                        pe.wait_ge(s["pt_sb"], k - 1)
                    for g in range(G):
                        m = pe.transpose(bank[4 + i % 2][0:S2, g * P:(g + 1) * P], prob[:, u, G * g + i, :], ident[:])
                    m.then_inc(s["pt_ps"], 1)

                def weigh(i):
                    pe.wait_ge(s["pt_sb"], HG * t + i + 1)
                    if i == 0 and t >= 2:
                        pe.wait_ge(s["x1_s"], t - 1)
                    for g in range(G):
                        m = pe.matmul(bank[6 + u][32 * g:32 * g + 32, 0:P],
                                      v_pad[:, b, g, i].rearrange("p a d -> p (a d)"), probT[0:S2, u, i, g, :],
                                      start=(i == 0), stop=(i == HG - 1))
                    return m

                turn(0)
                turn(1)
                for i in range(HG):
                    if i + 2 == HG and t + 3 < NT:
                        scores(t + 3)
                    m = weigh(i)
                    if i + 2 < HG:
                        turn(i + 2)
                m.then_inc(s["o_ps"], 1)
                pe.wait_ge(s["rwide_s"], t + 1)
                pe.transpose(bank[6 + u][:, P:2 * P], rsum_wide[:, u].rearrange("p h d -> p (h d)"), ident[:])\
                    .then_inc(s["r_ps"], 1)

            def project(t):
                pe.wait_ge(s["att_s"], t + 1)
                if t == 0:
                    pe.wait_ge(s["small_in"], 32)
                pe.matmul(bank[6 + t % 2][:, 2 * P:2 * P + D], attT[:, t % 2], wo_sb[:], start=True, stop=True).then_inc(s["y_ps"], 1)

            for n in range(3):
                scores(n)
                if n == 0:
                    rows_transposed(1)
                queries(n + 1)
            for t in range(2, NT + 3):
                if t < NT + 2:
                    attend(t - 2)
                if t >= 3:
                    project(t - 3)

            def logits(b):
                pe.wait_ge(s["z2_s"], TPB * (b + 1))
                for t in range(TPB):
                    m = pe.transpose(bank[b][:, t * P:(t + 1) * P], z2[:, b * TPB + t, :], ident[:])
                m.then_inc(s["x2_ps"], 1)
                pe.wait_ge(s["x2_s"], b + 1)
                for t in range(b * TPB, (b + 1) * TPB):
                    m = pe.matmul(bank[2 + 3 * b][:, t * E:(t + 1) * E], x2T[:, t * P:(t + 1) * P], router_sb[:],
                                  start=True, stop=True)
                m.then_inc(s["log_ps"], 1)

            def shared_gate(b):
                pe.matmul(bank[b], shgu_sb[:, 0:FS], x2T[:, b * S:(b + 1) * S], start=True, stop=True)\
                    .then_inc(s["shg_ps"], 1)

            def shared_up(b):
                pe.matmul(bank[4 + b], shgu_sb[:, FS:2 * FS], x2T[:, b * S:(b + 1) * S], start=True, stop=True)\
                    .then_inc(s["shu_ps"], 1)

            logits(0)
            logits(1)
            pe.wait_ge(s["sh_in"], 32)
            shared_gate(0)
            for t in range(NT):
                if t % TPB == 0:
                    pe.wait_ge(s["member_s"], t // TPB + 1)
                m = pe.matmul(bank[6][:, 0:E], ones[:], member[:, t, :], start=(t == 0), stop=(t == NT - 1))
                if t < NT - 1:
                    n = NT - 1 - t
                    pe.matmul(bank[3][:, (t + 1) * E:NT * E], ones[:], member[:, t:t + 1, :].to_broadcast([P, n, E]),
                              start=(t == 0), stop=False, skip_group_check=True)
            m.then_inc(s["cnt_ps"], 1)
            m = pe.matmul(bank[3][:, 0:NT * E], earlier[:], member[:].rearrange("p t e -> p (t e)"), start=False,
                          stop=True, skip_group_check=True)
            m.then_inc(s["rank_ps"], 1)
            shared_up(0)
            shared_gate(1)
            shared_up(1)
            pe.wait_ge(s["hotr_s"], 1)
            pe.wait_ge(s["hotv_s0"], 1)
            pe.wait_ge(s["hotv_s1"], 1)
            for n in range(PAIRS):
                m = pe.matmul(bank[7][:, 0:NV * JC], hot_r[:, n, :], hot_v[:, n].rearrange("p v j -> p (v j)"),
                              start=(n == 0), stop=(n == PAIRS - 1))
            m.then_inc(s["list_ps"], 1)

            def shared_down(b):
                pe.wait_ge(s["shh_s"], b + 1)
                pe.wait_ge(s["shc_s"], B)
                if b > 0:
                    pe.wait_ge(s["shared_s"], b)
                for t in range(TPB):
                    m = pe.matmul(bank[1][:, t * D:(t + 1) * D], sh_hT[:, (b * TPB + t) * P:(b * TPB + t + 1) * P],
                                  shdown_sb[:], start=True, stop=True)
                m.then_inc(s["shd_ps"], 1)

            def rows_tile(j, nth, r):
                pe.wait_ge(s[f"xg_s{r}"], nth * 16)
                if not isinstance(j, int) or j > 0:
                    pe.wait_ge(s["xf_s"], j)
                pe.transpose(bank[0][:, 0:P], xg[:, r], ident[:]).then_inc(s["xgT_ps"], 1)

            def products(out, high, low, first, n):
                pe.matmul(out, high, gu_high[:, bass.ds(first, n)], start=True, stop=False)
                pe.matmul(out, high, gu_low[:, bass.ds(first, n)], start=False, stop=False)
                return pe.matmul(out, low, gu_high[:, bass.ds(first, n)], start=False, stop=True)

            def gate_up_tile(j, u):
                e = pe.value_load(exp_i[0:1, bass.ds(j, 1)], min_val=0, max_val=E - 1)
                pe.wait_ge(s["xgT_s"], j + 1)
                products(bank[2 + u], xgT_hi[:, u], xgT_lo[:, u], e * (2 * F), F).then_inc(s["gu_ps"], 1)
                products(bank[4 + u], xgT_hi[:, u], xgT_lo[:, u], e * (2 * F) + F, F).then_inc(s["gu_ps"], 1)

            def down_tile(j, u):
                e = pe.value_load(exp_i[0:1, bass.ds(j, 1)], min_val=0, max_val=E - 1)
                pe.wait_ge(s["hT_s"], j + 1)
                if not isinstance(j, int) or j > 0:
                    pe.wait_ge(s["yy_s"], j)
                for c in range(FC):
                    m = pe.matmul(bank[7][:, 0:D], hidT[:, u, c * P:(c + 1) * P],
                                  down_sb[:, bass.ds(e * (FC * D) + c * D, D)], start=(c == 0), stop=(c == FC - 1))
                m.then_inc(s["yy_ps"], 1)

            def hidden_tile(j, u):
                pe.wait_ge(s["hid_s"], j + 1)
                if not isinstance(j, int) or j > 0:
                    pe.wait_ge(s["hT_s"], j)
                for c in range(FC):
                    m = pe.transpose(bank[6][:, c * P:(c + 1) * P], hid[:, u, c * P:(c + 1) * P], ident[:])
                m.then_inc(s["hT_ps"], 1)

            shared_down(0)
            pe.wait_ge(s["wlow_s"], E)
            pe.wait_ge(s["whigh_s"], 2 * E)
            pe.wait_ge(s["down_in"], 16 * E)
            pe.wait_ge(s["expert_s"], 1)

            def pe_step(j, r, n):
                late = isinstance(j, int) and j in (0, 1)
                if exists(j, 2) and not late:
                    rows_tile(j + 2, n + (r + 2) // RING + 1, (r + 2) % RING)
                if exists(j, 0):
                    gate_up_tile(j, r % 2)
                if late:
                    rows_tile(j + 2, n + (r + 2) // RING + 1, (r + 2) % RING)
                if isinstance(j, int) and j == 0:
                    shared_down(1)
                if exists(j, -2):
                    if isinstance(j, int) and j == 2:
                        pe.wait_ge(s["list_s"], 1)
                    down_tile(j - 2, r % 2)
                if exists(j, -1):
                    hidden_tile(j - 1, (r + 1) % 2)

            pipeline(pe, pe_step)

        @block.vector
        def _(dve):
            steps = [0]

            def step(ins):
                steps[0] += 1
                ins.then_inc(s["dstep"], 1)
                dve.wait_ge(s["dstep"], steps[0])

            def layer_stats(b):
                dve.wait_ge(s[f"x_in{b}"], 16)
                tiles = range(b * TPB, (b + 1) * TPB)
                for t in tiles:
                    dve.bn_stats(stats[:, t, :], x_sb[:, t, :]).then_inc(s["stats_s"], 1)
                for t in tiles:
                    dve.wait_ge(s["stats_s"], t + 1)
                    dve.bn_aggr(meanvar[:, t, :], stats[:, t, :]).then_inc(s["mv_s"], 1)
                dve.wait_ge(s["mv_s"], TPB * (b + 1))
                half = slice(b * TPB, (b + 1) * TPB)
                dve.tensor_scalar(veps[:, half], meanvar[:, half, 1], EPS, None, ALU.add).then_inc(s["veps_s"], 1)

            dve.memset(v_pad[:], 0.0).then_inc(s["vz_s"], 1)
            dve.memset(k_stack[:, :, :, :, S2:KP].bitcast(F32), 0.0).then_inc(s["kz_s"], 1)
            dve.memset(neg_hi[:, :, S2:KP].bitcast(F32), 0.0).then_inc(s["negz_s"], 1)
            dve.memset(neg_lo[:, :, S2:KP].bitcast(F32), 0.0).then_inc(s["negz_s"], 1)
            layer_stats(0)
            normalised(dve, 0)
            dve.wait_ge(s["bk_in"], 48)
            dve.tensor_scalar(bkq[:], bk_sb[:], QSCALE, None, ALU.mult).then_inc(s["bkq_s"], 1)
            layer_stats(1)
            dve.wait_ge(s["iota_s"], 2)
            step(dve.tensor_scalar(part_b[:], part_i[:], 3, HG - 1, ALU.logical_shift_right, ALU.bitwise_and))
            dve.tensor_tensor(headsel[:], part_b[:], iota_i[0:SP, 0:HG], ALU.is_equal).then_inc(s["headsel_s"], 1)
            dve.wait_ge(s["bq_in"], 48)
            dve.wait_ge(s["kf_s"], G)
            low = slice(2 * P // G, SP)
            dve.tensor_copy(k_hi[low], k_full[low]).then_inc(s["khi_s"], 1)
            dve.wait_ge(s["khi_s"], 1)
            dve.tensor_tensor(k_full[low], k_full[low], k_hi[low].bitcast(F32), ALU.subtract).then_inc(s["klo_s"], 1)
            dve.wait_ge(s["klo_s"], 1)
            dve.wait_ge(s["headsel_s"], 1)
            for g in range(G):
                dve.tensor_tensor(k_stack[:, g, 0, :, 0:S2], k_full[:, g, 0:1, :].to_broadcast([SP, HG, S2]),
                                  headsel[:].rearrange("p (i a) -> p i a", a=1).to_broadcast([SP, HG, S2]),
                                  ALU.mult).then_inc(s["ks_s0"], 1)

            def q_low(n):
                mid = slice(P // G, 2 * P // G)
                for g in range(G):
                    dve.wait_ge(s["qhi_s"], n * G + g + 1)
                    q_mid = q_stack[mid, g, n * QU:(n + 1) * QU]
                    dve.scalar_tensor_tensor(out=q_mid, in0=bank[4 + g][mid, 0:QU],
                                             scalar=bq_sb[mid, g:g + 1], in1=q_mid.bitcast(F32), op0=ALU.add,
                                             op1=ALU.subtract).then_inc(s["qlo_s"], 1)

            def values_padded():
                dve.wait_ge(s["v_ps"], 1)
                dve.wait_ge(s["v_in"], 32)
                dve.wait_ge(s["vz_s"], 1)
                for b in range(B):
                    for i in range(HG):
                        dve.tensor_tensor(
                            v_pad[:, b, :, i, i, :],
                            bank[1][0:S2, b * D:(b + 1) * D].rearrange("p (g i d) -> p g i d", g=G, i=HG)[:, :, i, :],
                            bv_sb[:].rearrange("p (g i d) -> p g i d", g=G, i=HG)[:, :, i, :], ALU.add)\
                            .then_inc(s["v_s"], 1)

            values_padded()
            q_low(0)
            normalised(dve, 1)

            def soft_sum(t):
                u = t % 2
                dve.wait_ge(s["exp_s"], t + 1)
                dve.tensor_reduce(sums[:, u, :], shifted[:, u], AX_X, ALU.add).then_inc(s["sum_s"], 1)

            def soft_recip(t):
                u = t % 2
                dve.wait_ge(s["sum_s"], t + 1)
                dve.reciprocal(rsum[:, u, :], sums[:, u, :]).then_inc(s["rsum_s"], 1)

            def soft_wide(t):
                u = t % 2
                dve.wait_ge(s["rsum_s"], t + 1)
                if t >= 2:
                    dve.wait_ge(s["r_ps"], t - 1)
                dve.tensor_copy(rsum_wide[:, u], rsum[:, u, :].rearrange("p (h a) -> p h a", a=1)
                                .to_broadcast([P, H, DH])).then_inc(s["rwide_s"], 1)

            def normalise(t):
                u = t % 2
                dve.wait_ge(s["r_sb"], t + 1)
                if t >= 2:
                    dve.wait_ge(s["y_ps"], t - 1)
                dve.tensor_tensor(attT[:, u], bank[6 + u][:, 0:P], rsumT[:, u], ALU.mult).then_inc(s["att_s"], 1)

            def residual(t):
                dve.wait_ge(s["y_ps"], t + 1)
                if t == 0:
                    dve.wait_ge(s["xb_s"], 1)
                dve.scalar_tensor_tensor(out=x1[:, t, :], in0=bank[6 + t % 2][:, 2 * P:2 * P + D], scalar=tanh_g[:, 0:1], in1=xb[:, t, :],
                                         op0=ALU.mult, op1=ALU.add).then_inc(s["x1_s"], 1)

            def stats_2(t):
                dve.wait_ge(s["x1_s"], t + 1)
                dve.bn_stats(stats2[:, t, :], x1[:, t, :]).then_inc(s["st2_s"], 1)

            score_view = quad[:, :, 0:HG * KP].rearrange("p g (i k) -> p g i k", i=HG)[:, :, :, 0:S2]

            def by_group(ap):
                return ap.rearrange("p (g i) k -> p g i k", g=G)

            def variance_2(b):
                half = slice(b * TPB, (b + 1) * TPB)
                for t in range(b * TPB, (b + 1) * TPB):
                    dve.wait_ge(s["st2_s"], t + 1)
                    dve.bn_aggr(meanvar2[:, t, :], stats2[:, t, :]).then_inc(s["mv2_s"], 1)
                dve.wait_ge(s["mv2_s"], TPB * (b + 1))
                dve.tensor_scalar(veps2[:, half], meanvar2[:, half, 1], 1.0 + EPS, EPS * EPS, ALU.mult, ALU.add)\
                    .then_inc(s["ve2_s"], 1)

            def normalised_2(b):
                dve.wait_ge(s["rr_s"], b + 1)
                for t in range(b * TPB, (b + 1) * TPB):
                    dve.tensor_scalar(z2[:, t, :], x1[:, t, :], meanvar2[:, t, 0:1], rr[:, t:t + 1],
                                      ALU.subtract, ALU.mult).then_inc(s["z2_s"], 1)

            for t in range(NT + 4):
                u = t % 2
                if t < NT:
                    if t == 2:
                        q_low(3)
                    dve.wait_ge(s["score_s"], t + 1)
                    dve.tensor_reduce(top[:, u, :].rearrange("p (g i) -> p g i", g=G), score_view, AX_X, ALU.max)\
                        .then_inc(s["max_s"], 1)
                if t >= 4:
                    residual(t - 4)
                if t < NT:
                    if t == 0:
                        dve.wait_ge(s["ks_s1"], G)
                    dve.wait_ge(s["max_s"], t + 1)
                    if t >= 2:
                        dve.wait_ge(s["prob_s"], t - 1)
                        dve.wait_ge(s["sum_s"], t - 1)
                    dve.tensor_tensor(by_group(shifted[:, u]), score_view,
                                      by_group(top[:, u, :].rearrange("p (h a) -> p h a", a=1).to_broadcast([P, H, S2])),
                                      ALU.subtract).then_inc(s["shift_s"], 1)
                if t < 2:
                    q_low(t + 1)
                if t == 0:
                    dve.wait_ge(s["tanh_s"], 1)
                    dve.wait_ge(s["gate_in"], 48)
                    dve.tensor_scalar(bo_g[:], bo_sb[:], tanh_g[:, 0:1], None, ALU.mult).then_inc(s["bog_s"], 1)
                if 3 <= t < NT + 3:
                    normalise(t - 3)
                if 1 <= t < NT + 1:
                    soft_sum(t - 1)
                if t >= 5:
                    stats_2(t - 5)
                if 1 <= t < NT + 1:
                    soft_recip(t - 1)
                if 1 <= t < NT + 1:
                    soft_wide(t - 1)
                if t == NT:
                    dve.wait_ge(s["iota_s"], 5)
                    dve.tensor_copy(iota_f[:], iota_i[:])
                    dve.tensor_copy(iota_b[:], iota_i[:])
                    dve.tensor_copy(part_f[:], part_col[:, 0:1])
                    dve.tensor_copy(tile_row_b[:], tile_row[:])
                    dve.tensor_copy(dump_f[:], dump_i[:]).then_inc(s["partf_s"], 1)
                if t == NT + 1:
                    variance_2(0)
                if t == NT + 2:
                    normalised_2(0)
            stats_2(NT - 1)

            variance_2(1)
            normalised_2(1)

            for b in range(B):
                tiles = range(b * TPB, (b + 1) * TPB)
                half = slice(b * TPB, (b + 1) * TPB)
                dve.wait_ge(s["log_ps"], b + 1)
                step(dve.tensor_copy(logit[:, half], bank[2 + 3 * b][:, b * TPB * E:(b + 1) * TPB * E]
                                     .rearrange("p (t e) -> p t e", t=TPB)))
                for t in tiles:
                    m = dve.max(best[:, t, :], logit[:, t, :])
                step(m)
                for t in tiles:
                    m = dve.max_index(best_i[:, t, :], best[:, t, :], logit[:, t, :])
                dve.tensor_tensor(gap[:, half], best[:, half, 1], best[:, half, 0], ALU.subtract).then_inc(s["gap_s"], 1)
                step(m)
                step(dve.tensor_copy(choice_f[:, :, half], best_i[:, half, 0:TOPK].rearrange("p t k -> p k t")))
                for k in range(TOPK):
                    m = dve.tensor_tensor(onehot[:, k, half], iota_f[:, 0:E].rearrange("p (a e) -> p a e", a=1)
                                          .to_broadcast([P, TPB, E]),
                                          choice_f[:, k, half].rearrange("p (t a) -> p t a", a=1)
                                          .to_broadcast([P, TPB, E]), ALU.is_equal)
                step(m)
                dve.tensor_tensor(member[:, half], onehot[:, 0, half], onehot[:, 1, half], ALU.add)\
                    .then_inc(s["member_s"], 1)

            def shared_clip(b):
                dve.wait_ge(s["shg_ps"], b + 1)
                dve.tensor_scalar(sh_gate[:, b * S:(b + 1) * S], bank[b], -10.0, 10.0, ALU.max, ALU.min)\
                    .then_inc(s["shc_s"], 1)

            shared_clip(0)

            def shared_hidden(b):
                c = slice(b * S, (b + 1) * S)
                dve.wait_ge(s["shu_ps"], b + 1)
                dve.wait_ge(s["shsilu_s"], b + 1)
                dve.tensor_tensor(sh_hT[:, c], bank[4 + b], sh_silu[:, c], ALU.mult).then_inc(s["shh_s"], 1)

            def mark(ins):
                steps[0] += 1
                ins.then_inc(s["dstep"], 1)
                return steps[0]

            def after(count):
                dve.wait_ge(s["dstep"], count)

            by_pair = onehot[:].rearrange("p k t e -> p (k t) e")
            dve.wait_ge(s["cnt_ps"], 1)
            counted = mark(dve.tensor_scalar(cnt_i[:], bank[6][:, 0:E], float(P - 1), None, ALU.add))
            dve.wait_ge(s["rank_ps"], 1)
            ranked = mark(dve.tensor_tensor(
                rank_te[:].rearrange("p (k t) e -> p k (t e)", k=TOPK), onehot[:].rearrange("p k t e -> p k (t e)"),
                bank[3][:, 0:NT * E].rearrange("p (a n) -> p a n", a=1).to_broadcast([P, TOPK, NT * E]), ALU.mult))
            after(counted)
            tiled = mark(dve.tensor_scalar(tiles_i[:], cnt_i[:], 7, None, ALU.logical_shift_right))
            after(ranked)
            ranked = mark(dve.tensor_reduce(rank_f[:], rank_te[:], AX_X, ALU.add))
            after(tiled)
            tiled = mark(dve.tensor_copy(tiles_f[:], tiles_i[:]))
            after(ranked)
            ranked = mark(dve.tensor_copy(rank_i[:], rank_f[:]))
            after(tiled)
            dve.wait_ge(s["const"], 7)
            tiled = mark(dve.tensor_tensor(tiles_sq[:], upto[:], tiles_f[:].rearrange("p (a e) -> p a e", a=1)
                                           .to_broadcast([P, E, E]), ALU.mult))
            after(ranked)
            nth = mark(dve.tensor_scalar(nth_i[:], rank_i[:], 7, None, ALU.logical_shift_right))
            after(tiled)
            tiled = mark(dve.tensor_reduce(tiles_incl[:], tiles_sq[:], AX_X, ALU.add))
            after(nth)
            nth = mark(dve.tensor_copy(nth_f[:], nth_i[:]))
            after(tiled)
            tiled = mark(dve.tensor_tensor(tiles_excl[:], tiles_incl[:], tiles_f[:], ALU.subtract))
            in_tile = mark(dve.tensor_scalar(row_i[:], rank_i[:], P - 1, None, ALU.bitwise_and))
            after(tiled)
            first = mark(dve.tensor_tensor(first_te[:], by_pair, tiles_excl[:].rearrange("p (a e) -> p a e", a=1)
                                           .to_broadcast([P, PAIRS, E]), ALU.mult))
            after(in_tile)
            in_tile = mark(dve.tensor_copy(sr_b[:], row_i[:]))
            after(first)
            first = mark(dve.tensor_reduce(first_f[:], first_te[:], AX_X, ALU.add))
            after(first)
            tile_of = mark(dve.tensor_tensor(sj_b[:], first_f[:], nth_f[:], ALU.add))
            after(tile_of)
            dve.tensor_tensor(hot_j[:], iota_b[:, 0:JC].rearrange("p (a j) -> p a j", a=1).to_broadcast([P, PAIRS, JC]),
                              sj_b[:].rearrange("p (n a) -> p n a", a=1).to_broadcast([P, PAIRS, JC]), ALU.is_equal)\
                .then_inc(s["hotj_s"], 1)
            dve.tensor_tensor(hot_r[:], iota_b[:].rearrange("p (a r) -> p a r", a=1).to_broadcast([P, PAIRS, P]),
                              sr_b[:].rearrange("p (n a) -> p n a", a=1).to_broadcast([P, PAIRS, P]), ALU.is_equal)\
                .then_inc(s["hotr_s"], 1)
            shared_clip(1)
            dve.wait_ge(s["list_ps"], 1)
            step(dve.tensor_copy(lists[:], bank[7][:, 0:NV * JC].rearrange("p (v j) -> p v j", v=NV)))
            step(dve.tensor_tensor(row_li[:], lists[:, 0, :], lists[:, 1, :], ALU.add))
            dve.tensor_scalar(gidx[:], row_li[:], TOK - 1, None, ALU.bitwise_and).then_inc(s["list_s"], 1)
            step(dve.scalar_tensor_tensor(out=unused[:], in0=lists[:, 1, :], scalar=0.0, in1=dump_f[:],
                                          op0=ALU.is_equal, op1=ALU.mult))
            dve.scalar_tensor_tensor(out=sidx[:], in0=row_li[:], scalar=-float(TOPK * TOK), in1=unused[:],
                                     op0=ALU.add, op1=ALU.add).then_inc(s["list_s"], 1)
            shared_hidden(0)
            step(dve.tensor_tensor(past[:], tiles_incl[:].rearrange("p (a e) -> p a e", a=1).to_broadcast([P, JC, E]),
                                   iota_f[:, 0:JC].rearrange("p (j a) -> p j a", a=1).to_broadcast([P, JC, E]),
                                   ALU.is_le))
            step(dve.tensor_reduce(exp_f[:], past[:], AX_X, ALU.add))
            step(dve.tensor_scalar(exp_c[:], exp_f[:], float(E - 1), None, ALU.min))
            dve.tensor_copy(exp_i[:], exp_c[:]).then_inc(s["expert_s"], 1)

            shared_hidden(1)
            def rows_full(j, u):
                dve.wait_ge(s["xgT_ps"], j + 1)
                dve.tensor_scalar(xgT[:, u], bank[0][:, 0:P], col_sb[:, 0:1], col_sb[:, 1:2], ALU.mult, ALU.add)\
                    .then_inc(s["xf_s"], 1)

            def rows_low(j, u):
                dve.wait_ge(s["xf_s"], j + 1)
                dve.wait_ge(s["xh_s"], j + 1)
                dve.tensor_tensor(xgT_lo[:, u], xgT[:, u], xgT_hi[:, u].bitcast(F32), ALU.subtract)\
                    .then_inc(s["xgT_s"], 1)

            def clip_tile(j, u):
                dve.wait_ge(s["gu_ps"], j * 2 + 1)
                dve.tensor_scalar(gate[:, u], bank[2 + u], -10.0, 10.0, ALU.max, ALU.min).then_inc(s["clip_s"], 1)

            def hid_tile(j, u):
                dve.wait_ge(s["silu_s"], j + 1)
                dve.wait_ge(s["gu_ps"], j * 2 + 2)
                dve.tensor_tensor(hid[:, u], bank[4 + u], silu[:, u], ALU.mult).then_inc(s["hid_s"], 1)

            def dve_step(j, r, n):
                if exists(j, 0):
                    clip_tile(j, r % 2)
                if exists(j, 2):
                    rows_full(j + 2, r % 2)
                if exists(j, 0):
                    hid_tile(j, r % 2)
                if exists(j, 2):
                    rows_low(j + 2, r % 2)
                if isinstance(j, int) and j == 3:
                    dve.wait_ge(s["egap_s"], 1)
                    step(dve.tensor_scalar(egap1[:], egap[:], 1.0, None, ALU.add))
                    step(dve.reciprocal(wgt[:, 0, :], egap1[:]))
                    step(dve.tensor_tensor(wgt[:, 1, :], wgt[:, 0, :], egap[:], ALU.mult))
                    dve.tensor_scalar(wgt_g[:], wgt[:], tanh_g[:, 1:2], None, ALU.mult).then_inc(s["wgt_s"], 1)

            dve.wait_ge(s["col_in"], 32)
            pipeline(dve, dve_step)

            dve.wait_ge(s["base_s"], 1)
            dve.wait_ge(s["wgt_s"], 1)

            def first_choice(b):
                dve.wait_ge(s[f"chosen_s{b}0"], 16)
                for t in range(b * TPB, (b + 1) * TPB):
                    dve.scalar_tensor_tensor(out=sum1[:, t, :], in0=chosen[:, 0, t, :], scalar=wgt_g[:, 0, t:t + 1],
                                             in1=base[:, t, :], op0=ALU.mult, op1=ALU.add).then_inc(s["sum1_s"], 1)

            def second_choice(b):
                half = slice(b * TPB, (b + 1) * TPB)
                dve.wait_ge(s["second_s"], TPB * (b + 1))
                dve.wait_ge(s["sum1_s"], TPB * (b + 1))
                dve.tensor_tensor(result[:, half], sum1[:, half], chosen[:, 1, half], ALU.add).then_inc(s["result_s"], 1)

            for b in range(B):
                first_choice(b)
            for b in range(B):
                second_choice(b)


_INS = ['x', 'ctx_1024', 'fside_BxSxS2_0', 'mask_BxSxS2_ik1', 'g_xattn', 'g_ffn', 'L0_xattn_wq_k', 'L0_xattn_wq_b',
        'L0_xattn_wk_k', 'L0_xattn_wk_b', 'L0_xattn_wv_k', 'L0_xattn_wv_b', 'L0_xattn_wo_k', 'L0_xattn_wo_b',
        'L0_ffn_ln_gamma', 'L0_ffn_ln_beta', 'L0_ffn_router_w', 'L0_ffn_gate_up_w', 'L0_ffn_down_w',
        'L0_ffn_shared_gate_up_w', 'L0_ffn_shared_down_w']


def kernel(**inputs):
    import numpy as _np
    import concourse.bacc as _bacc
    from concourse import mybir as _mybir
    from concourse.bass_utils import run_bass_kernel_spmd as _run

    nc = _bacc.Bacc("TRN2", target_bir_lowering=False, num_devices=1)
    arrays, args = {}, []
    for name in _INS:
        a = _np.ascontiguousarray(inputs[name])
        arrays[f"in_{name}_dram"] = a
        args.append(nc.dram_tensor(f"in_{name}_dram", a.shape, _mybir.dt.from_np(a.dtype), kind="ExternalInput").ap())
    shape = inputs["x"].shape
    args.append(nc.dram_tensor("out_0_dram", shape, _mybir.dt.float32, kind="ExternalOutput").ap())
    gated_block(nc, *args)
    r = _run(nc, [arrays], core_ids=[0])
    return r.results[0]["out_0_dram"]
```
